# Optimizing a Trainium2 kernel written in Bass

```python
import numpy as np
import jax
import jax.numpy as jnp

def _softmax(x, axis=-1):
    return jax.nn.softmax(x, axis=axis)

def _gelu(x):
    return jax.nn.gelu(x, approximate=True)

def _silu(x):
    return jax.nn.silu(x)

def _sigmoid(x):
    return jax.nn.sigmoid(x)

def _layernorm(x, axis=-1, eps=1e-05):
    m = jnp.mean(x, axis=axis, keepdims=True)
    v = jnp.var(x, axis=axis, keepdims=True)
    return (x - m) / jnp.sqrt(v + eps)

def _scatter_add(tgt, idx, src, axis=0):
    return tgt.at[idx].add(src)

def _segment_sum(src, seg, n):
    return jax.ops.segment_sum(src, seg, n)
kernel_name = 'mk_gnn_resnorm_d2_gnn_r8_638852'

def setup_inputs(seed: int=0):
    np.random.seed(seed)
    _w = jnp.asarray

    def _rec_inputs():
        import jax
        import jax.numpy as jnp
        _gk = jax.random.key(seed)
        x = -0.000202 + 1 * jax.random.normal(jax.random.fold_in(_gk, 1), (6250, 128), jnp.float32)
        src = jax.random.randint(jax.random.fold_in(_gk, 2), (200000,), 0, 6250, jnp.int32)
        dst = jax.random.randint(jax.random.fold_in(_gk, 3), (200000,), 0, 6250, jnp.int32)
        _o = jnp.argsort(dst, stable=True)
        src = src[_o]
        dst = dst[_o]
        edge_type_200 = jax.random.randint(jax.random.fold_in(_gk, 13), (200000,), 0, 200, jnp.int32)
        return (x, src, dst, edge_type_200)
    x, src, dst, edge_type_200 = _rec_inputs()

    def _L0_gnn_setup():
        import jax, jax.numpy as jnp
        import numpy as np
        N, E, D, R = (6250, 100000, 128, 200)
        key = jax.random.key(seed)
        ks = jax.random.split(key, 8)
        h = jax.random.normal(ks[0], (N, D), jnp.float32)
        emb_rel = jax.random.normal(ks[1], (R, D), jnp.float32)
        loop_weight = jax.random.normal(ks[2], (D, D), jnp.float32) * 0.05
        attn_fc_w = jax.random.normal(ks[3], (D, 3 * D), jnp.float32) * 0.05
        attn_fc2_w = jax.random.normal(ks[4], (1, D), jnp.float32) * 0.05
        src = jax.random.randint(ks[5], (E,), 0, N)
        dst = jax.random.randint(ks[6], (E,), 0, N)
        etype = jax.random.randint(ks[7], (E,), 0, R)
        return {'h': h, 'emb_rel': emb_rel, 'loop_weight': loop_weight, 'attn_fc_w': attn_fc_w, 'attn_fc2_w': attn_fc2_w, 'src': src, 'dst': dst, 'etype': etype}
    _L0_gnn_all = _L0_gnn_setup()
    _L0_gnn_in = {k: v for k, v in _L0_gnn_all.items() if k in ('emb_rel', 'loop_weight', 'attn_fc_w', 'attn_fc2_w')}
    del _L0_gnn_all

    def _L1_gnn_setup():
        import jax, jax.numpy as jnp
        import numpy as np
        N_NODES = 12500
        N_EDGES = 80000
        N_RELS = 200
        D = 128
        RRELU_SLOPE = (1.0 / 8.0 + 1.0 / 3.0) / 2.0

        def rrelu(x):
            return jnp.where(x >= 0, x, x * RRELU_SLOPE)

        def _layer(h, e_h, src, dst, iso_mask, norm, W_r, W_sl, W_el):
            self_msg = jnp.where(iso_mask[:, None], h @ W_el, h @ W_sl)
            msg = (e_h + h[src]) @ W_r
            agg = jax.ops.segment_sum(msg, dst, num_segments=h.shape[0])
            return rrelu(agg * norm + self_msg)
        key = jax.random.key(seed)
        ks = jax.random.split(key, 12)
        inp = {'ent_embed': jax.random.normal(ks[0], (N_NODES, D), dtype=jnp.float32), 'rel_embed': jax.random.normal(ks[1], (N_RELS, D), dtype=jnp.float32), 'norm': jax.random.uniform(ks[2], (N_NODES, 1), dtype=jnp.float32), 'src': jax.random.randint(ks[3], (N_EDGES,), 0, N_NODES), 'dst': jax.random.randint(ks[4], (N_EDGES,), 0, N_NODES), 'rel_id': jax.random.randint(ks[5], (N_EDGES,), 0, N_RELS)}
        scale = 1.0 / np.sqrt(D)
        for i, name in enumerate(['W_r1', 'W_sl1', 'W_el1', 'W_r2', 'W_sl2', 'W_el2']):
            inp[name] = jax.random.uniform(ks[6 + i], (D, D), dtype=jnp.float32, minval=-scale, maxval=scale)
        return inp
    _L1_gnn_all = _L1_gnn_setup()
    _L1_gnn_in = {k: v for k, v in _L1_gnn_all.items() if k in ('rel_embed', 'W_r1', 'W_sl1', 'W_el1', 'W_r2', 'W_sl2', 'W_el2')}
    del _L1_gnn_all
    return {'x': x, 'src': src, 'dst': dst, 'edge_type_200': edge_type_200, 'L0_gnn_emb_rel': _L0_gnn_in['emb_rel'], 'L0_gnn_loop_weight': _L0_gnn_in['loop_weight'], 'L0_gnn_attn_fc_w': _L0_gnn_in['attn_fc_w'], 'L0_gnn_attn_fc2_w': _L0_gnn_in['attn_fc2_w'], 'L1_gnn_rel_embed': _L1_gnn_in['rel_embed'], 'L1_gnn_W_r1': _L1_gnn_in['W_r1'], 'L1_gnn_W_sl1': _L1_gnn_in['W_sl1'], 'L1_gnn_W_el1': _L1_gnn_in['W_el1'], 'L1_gnn_W_r2': _L1_gnn_in['W_r2'], 'L1_gnn_W_sl2': _L1_gnn_in['W_sl2'], 'L1_gnn_W_el2': _L1_gnn_in['W_el2']}

def reference(x, src, dst, edge_type_200, L0_gnn_emb_rel, L0_gnn_loop_weight, L0_gnn_attn_fc_w, L0_gnn_attn_fc2_w, L1_gnn_rel_embed, L1_gnn_W_r1, L1_gnn_W_sl1, L1_gnn_W_el1, L1_gnn_W_r2, L1_gnn_W_sl2, L1_gnn_W_el2):
    import jax
    import jax.numpy as jnp

    def _L0_gnn_ref(h, emb_rel, loop_weight, attn_fc_w, attn_fc2_w, src, dst, etype):
        import jax, jax.numpy as jnp
        import numpy as np
        N, E, D, R = (6250, 100000, 128, 200)
        num_nodes = h.shape[0]
        Ws, Wd, Wr = jnp.split(attn_fc_w, 3, axis=1)
        hs = h[src]
        a = hs @ Ws.T + h[dst] @ Wd.T + emb_rel[etype] @ Wr.T
        e = jax.nn.leaky_relu((a @ attn_fc2_w.T)[:, 0], 0.01)
        m = jax.ops.segment_max(e, dst, num_segments=num_nodes)
        w = jnp.exp(e - m[dst])
        denom = jax.ops.segment_sum(w, dst, num_segments=num_nodes)
        alpha = w / denom[dst]
        agg = jax.ops.segment_sum(alpha[:, None] * hs, dst, num_segments=num_nodes)
        deg = jax.ops.segment_sum(jnp.ones_like(e), dst, num_segments=num_nodes)
        agg = jnp.where(deg[:, None] > 0, agg, h)
        return agg + h @ loop_weight

    def _L1_gnn_ref(ent_embed, rel_embed, norm, src, dst, rel_id, W_r1, W_sl1, W_el1, W_r2, W_sl2, W_el2):
        import jax, jax.numpy as jnp
        import numpy as np
        N_NODES = 12500
        N_EDGES = 80000
        N_RELS = 200
        D = 128
        RRELU_SLOPE = (1.0 / 8.0 + 1.0 / 3.0) / 2.0

        def rrelu(x):
            return jnp.where(x >= 0, x, x * RRELU_SLOPE)

        def _layer(h, e_h, src, dst, iso_mask, norm, W_r, W_sl, W_el):
            self_msg = jnp.where(iso_mask[:, None], h @ W_el, h @ W_sl)
            msg = (e_h + h[src]) @ W_r
            agg = jax.ops.segment_sum(msg, dst, num_segments=h.shape[0])
            return rrelu(agg * norm + self_msg)
        num_nodes = ent_embed.shape[0]
        e_h = rel_embed[rel_id]
        in_deg = jax.ops.segment_sum(jnp.ones_like(dst), dst, num_segments=num_nodes)
        iso_mask = in_deg == 0
        h = ent_embed
        for W_r, W_sl, W_el in [(W_r1, W_sl1, W_el1), (W_r2, W_sl2, W_el2)]:
            h = _layer(h, e_h, src, dst, iso_mask, norm, W_r, W_sl, W_el)
        return h
    deg = jnp.maximum(jax.ops.segment_sum(jnp.ones(dst.shape, jnp.float32), dst, num_segments=6250), 1.0)
    deg_isqrt = deg ** (-0.5)
    x = _layernorm(x + _L0_gnn_ref(x, L0_gnn_emb_rel, L0_gnn_loop_weight, L0_gnn_attn_fc_w, L0_gnn_attn_fc2_w, src, dst, edge_type_200), axis=-1)
    x = _layernorm(x + _L1_gnn_ref(x, L1_gnn_rel_embed, deg_isqrt[:, None], src, dst, edge_type_200, L1_gnn_W_r1, L1_gnn_W_sl1, L1_gnn_W_el1, L1_gnn_W_r2, L1_gnn_W_sl2, L1_gnn_W_el2), axis=-1)
    return x

_drawn_inputs = setup_inputs


def setup_inputs(seed=0):
    import zlib

    import numpy as np

    out = dict(_drawn_inputs(seed))
    spreads = {}
    factors = {}
    for name, (base, spread) in spreads.items():
        noise = np.random.default_rng([zlib.crc32(name.encode()), seed]).standard_normal(out[name].shape)
        drawn = base * np.exp(spread * noise) if base else spread * noise
        out[name] = jnp.asarray(drawn.astype(out[name].dtype))
    for name, factor in factors.items():
        out[name] = (out[name] * factor).astype(out[name].dtype)
    return out
```

```python
from contextlib import ExitStack, contextmanager

import concourse.bass as bass
from concourse import mybir

F32 = mybir.dt.float32
BF16 = mybir.dt.bfloat16
I32 = mybir.dt.int32
ALU = mybir.AluOpType
ACT = mybir.ActivationFunctionType
AX = mybir.AxisListType.X

P = 128
N, D, R, E = 6250, 128, 200, 200000
TN = 125
NT = N // TN
PAIRS = NT // 2
C = 34
HC = C // 2
WIN = C * P
SAMP = 32
EP = 125
EW = E // EP
NS = EW // SAMP
NBMAX = -(-E // WIN)
PADW = -(-(NBMAX * WIN + WIN) // P)
PAD = P * PADW
NODST = 16383.0
HW = 132
GRP = 4
NG = -(-C // GRP)
L0_LINKS = 35
SLOPE = (1.0 / 8.0 + 1.0 / 3.0) / 2.0
EPS = 1e-5
assert EP * EW == E and NS * SAMP == EW and NT * TN == N and PAIRS * 2 == NT


class Chain:

    def __init__(self, eng, sem, passed):
        self.passed = passed
        self.eng, self.sem, self.base, self.count = eng, sem, 0, 0

    def link(self, ins):
        ins.then_inc(self.sem, 1)
        self.count += 1
        self.eng.wait_ge(self.sem, self.base + self.count)

    def link_alone(self, ins):
        self.link(ins)
        self.eng.nop().then_inc(self.passed, 1)

    @contextmanager
    def turns(self, turn, each, turns):
        outer = self.base + self.count
        self.base, self.count = outer + turn * each, 0
        yield
        assert self.count == each, (self.count, each)
        self.base, self.count = outer + turns * each, 0


def build(nc, x, src, dst, etype, emb_rel, loop_w, fc_w, fc2_w, rel_emb, W_r, W_sl, W_el, out):
    ctx = ExitStack()
    with ctx:
        def sb(name, shape, dt=F32):
            return ctx.enter_context(nc.sbuf_tensor(name, shape, dt))

        def sem(name):
            return ctx.enter_context(nc.semaphore(name))

        def dram(name, shape, dt):
            return nc.dram_tensor(name, shape, dt, kind="Internal").ap()

        srcp, dstp, etp = (dram(n, (E + PAD,), I32) for n in ("src_padded", "dst_padded", "etype_padded"))
        table = [dram("rows0", (N, HW), F32), dram("rows1", (N, D), F32), dram("rows2", (N, D), F32)]

        xs = sb("xs", [P, NT, HW])
        res = sb("res", [P, NT, D])
        ys = sb("ys", [P, NT, D])
        erel = sb("erel", [P, NT, D])
        ssd = sb("ssd", [P, NT, 2])
        mv = sb("mv", [P, NT, 2])
        rstd = sb("rstd", [P, NT])
        degs = sb("degs", [P, NT])
        norm = sb("norm", [P, NT])
        iso = sb("iso", [P, NT])
        niso = sb("niso", [P, NT])
        rows = sb("rows", [P, 2, C, HW])
        srcw = sb("srcw", [P, 2, C], I32)
        dstw = sb("dstw", [P, 2, C], I32)
        etw = sb("etw", [P, 2, C], I32)
        etf = sb("etf", [P, C])
        dl = sb("dl", [P, C])
        rv = sb("rv", [P, C])
        u = sb("u", [P, C])
        up = sb("up", [P, C])
        z = sb("z", [P, C + 1])
        z2 = sb("z2", [P, C])
        wexp = sb("wexp", [P, C + 1])
        hot = sb("hot", [P, C, P])
        hotb = sb("hotb", [P, C, P], BF16)
        hotT = sb("hotT", [P, C, P], BF16)
        toh = sb("toh", [P, C, R], BF16)
        gmax = sb("gmax", [P, NG])
        bmax = sb("bmax", [P, 1])
        mrun = sb("mrun", [P, 2])
        mold = sb("mold", [P, 4])
        bm = sb("bm", [P, 2])
        bmr = sb("bmr", [P, 2, 2])
        bm3 = sb("bm3", [P, 3, 2], BF16)
        look = sb("look", [P, C, 2])
        acc = sb("acc", [P, 2, HW])
        cacc = sb("cacc", [P, 2, R])
        cT = sb("cT", [P, 2, P])
        fin = sb("fin", [P, 8])
        stat = sb("stat", [P, 6])
        agg = sb("agg", [P, D])
        aggT = sb("aggT", [P, P])
        tmp = sb("tmp", [P, 2, D])
        stage = sb("stage", [P, 2, D])
        nT = sb("nT", [P, 2, P])
        iota_i = sb("iota_i", [P, 256], I32)
        iota = sb("iota", [P, 256])
        iotab = sb("iotab", [P, 256], BF16)
        thr_i = sb("thr_i", [P, NT + 1], I32)
        thr = sb("thr", [P, NT + 1])
        jw_i = sb("jw_i", [P, NBMAX], I32)
        jw = sb("jw", [P, NBMAX])
        later = sb("later", [P, NBMAX])
        ident = sb("ident", [P, P])
        ones = sb("ones", [P, P])
        w2 = sb("w2", [P, 1])
        v3 = sb("v3", [P, 3])
        rrow = sb("rrow", [P, R])
        relr = sb("relr", [P, 2, D])
        wr = sb("wr", [P, 2, D])
        wself = sb("wself", [P, 2, 2 * D])
        epst = sb("epst", [P, 1])
        plan = sb("plan", [P, 64])
        plan2 = sb("plan2", [P, 64])
        plan_i = sb("plan_i", [1, 64], I32)
        part = sb("part", [P, NT + 2])
        lows = sb("lows", [P, 4])
        low = sb("low", [P, 2])
        padz = hot[:, :, :].rearrange("p a b -> p (a b)").bitcast(I32)
        early = hotb[:, :, :].rearrange("p a b -> p (a b)").bitcast(F32)
        wfc, vrb, embT, wloop = early[:, 0:384], early[:, 384:512], early[:, 512:712], early[:, 712:842]
        embr = early[:, 842:1098].rearrange("p (a f) -> p a f", a=2)
        scr = rows[:, :, :, :].rearrange("p s a b -> p (s a b)")
        dall = scr[:, 5696:5696 + 2 * EW].bitcast(I32)

        bank = [ctx.enter_context(nc.psum_tensor(f"bank{i}", [P, 512], F32)) for i in range(8)]

        S = {}

        def s(name):
            if name not in S:
                S[name] = sem(name)
            return S[name]

        for name in ("xs_zero ld_w loads_x ld_dst ld_next out_stored pads edges iotas consts plan nb_ready v3_ready vrb_ready vsd emb_t emb_c rrow_ps "
                     "part_ready cnt_ps lowT low_ps low_in low_c dve_seq dve_passed pool_passed pool_c "
                     "x_ready xt_ready mx_done mt_done bm_ready lk_ready d_ready w_ready oh_ready mask_ready wm_ready "
                     "acc_ready c_ready cc_ready ct_ready ctc_ready er_ready er_done st_out").split():
            s(name)
        win = [sem(f"win{p}") for p in range(2)]
        win_free = [sem(f"win_free{p}") for p in range(2)]
        gath = [[sem(f"gath{p}{j}") for j in range(2)] for p in range(2)]
        lay = [{n: sem(f"{n}_{k}") for n in ("hot_ready", "acc_ready", "s_ready", "sT_ready", "sTc_ready", "o_ready")}
               | {"win": [sem(f"win_{k}{p}") for p in range(2)],
                  "win_free": [sem(f"win_free_{k}{p}") for p in range(2)],
                  "gath": [[sem(f"gath_{k}{p}{j}") for j in range(2)] for p in range(2)]} for k in range(2)]
        ph = [{n: sem(f"{n}_ph{k}") for n in ("nsrc", "staged", "tp", "xt", "mp", "nd", "var", "rs", "stored")} for k in range(3)]

        block = ctx.enter_context(nc.Block())

        def windows(eng, nb):
            @contextmanager
            def loop():
                with eng.Fori(0, PAIRS) as i:
                    with eng.Fori(0, nb) as b:
                        yield i, b, i * nb + b
            return loop()

        def at(t, q, i):
            return t[:, bass.ds(2 * i + q, 1), :].rearrange("p a f -> p (a f)")

        def window_list(a, start):
            return a[bass.ds(start, WIN)].rearrange("(p c) -> p c", c=C)

        @block.sync
        def _(sp):
            sp.dma_start(dall[0:EP, 0:EW], dst.rearrange("(p e) -> p e", p=EP)).then_inc(s("ld_dst"), 16)
            sp.wait_ge(s("xs_zero"), 1)
            sp.dma_start(xs[0:TN, :, 0:D], x.rearrange("(t p) f -> p t f", p=TN)).then_inc(s("loads_x"), 16)
            for a, b in ((src, srcp), (dst, dstp), (etype, etp)):
                sp.dma_start(b[0:E].rearrange("(p e) -> p e", p=EP), a.rearrange("(p e) -> p e", p=EP)).then_inc(s("edges"), 16)
            sp.wait_ge(s("pads"), 1)
            sp.dma_start(srcp[E:E + PAD].rearrange("(p e) -> p e", p=P), padz[:, 0:PADW]).then_inc(s("edges"), 16)
            sp.dma_start(etp[E:E + PAD].rearrange("(p e) -> p e", p=P), padz[:, 0:PADW]).then_inc(s("edges"), 16)
            sp.wait_ge(s("pads"), 2)
            sp.dma_start(dstp[E:E + PAD].rearrange("(p e) -> p e", p=P), padz[:, PADW:2 * PADW]).then_inc(s("edges"), 16)
            sp.wait_ge(s("edges"), 96)
            sp.dma_start(dall[0:EP, EW:2 * EW], dstp[1:E + 1].rearrange("(p e) -> p e", p=EP)).then_inc(s("ld_next"), 16)
            sp.wait_ge(ph[0]["nd"], NT + 2)
            sp.dma_start(table[0].rearrange("(t p) f -> p t f", p=TN), xs[0:TN, :, :]).then_inc(ph[0]["stored"], 16)
            sp.wait_ge(s("nb_ready"), 1)
            nb = sp.value_load(plan_i[0:1, NT:NT + 1], min_val=1, max_val=NBMAX)

            def load_windows(win, free):
                with windows(sp, nb) as (i, b, n):
                    for p in range(2):
                        first = sp.value_load(plan_i[0:1, bass.ds(2 * i + p, 1)], min_val=0, max_val=E)
                        sp.wait_ge(free[p], n + 1)
                        for a, w in ((srcp, srcw), (dstp, dstw), (etp, etw)):
                            sp.dma_start(w[:, p, :], window_list(a, first + b * WIN)).then_inc(win[p], 16)

            load_windows(win, win_free)
            for k in range(2):
                sp.wait_ge(ph[k + 1]["nsrc"], NT)
                sp.dma_start(table[k + 1].rearrange("(t p) f -> p t f", p=TN),
                             (xs[0:TN, :, 0:D] if k == 0 else ys[0:TN, :, :])).then_inc(ph[k + 1]["stored"], 16)
                load_windows(lay[k]["win"], lay[k]["win_free"])
            sp.wait_ge(s("st_out"), 1)
            sp.dma_start(out.rearrange("(t p) f -> p t f", p=TN), ys[0:TN, :, :]).then_inc(s("out_stored"), 16)
            sp.wait_ge(s("out_stored"), 16)

        @block.gpsimd
        def _(pool):
            pool.memset(padz[:, 0:PADW], 0).then_inc(s("pads"), 1)
            pool.memset(padz[:, PADW:2 * PADW], int(NODST)).then_inc(s("pads"), 1)
            pool.iota(iota_i[:], [[1, 256]], base=0, channel_multiplier=0).then_inc(s("iotas"), 1)
            pool.iota(thr_i[:], [[TN, NT + 1]], base=0, channel_multiplier=0).then_inc(s("iotas"), 1)
            pool.iota(jw_i[:], [[WIN, NBMAX]], base=0, channel_multiplier=0).then_inc(s("iotas"), 1)
            pool.memset(ident[:], 0.0).then_inc(s("pool_c"), 1)
            pool.wait_ge(s("pool_c"), 1)
            pool.affine_select(out=ident[:], in_=ident[:], compare_op=ALU.not_equal, fill=1.0, base=0,
                               pattern=[[-1, P]], channel_multiplier=1).then_inc(s("consts"), 1)
            for p in range(2):
                pool.nop().then_inc(win_free[p], 1)
                for k in range(2):
                    pool.nop().then_inc(lay[k]["win_free"][p], 1)
            for k in range(3):
                pool.nop().then_inc(ph[k]["tp"], 2)

            def stage_rows(k, source):
                with pool.Fori(0, PAIRS) as i:
                    for q in range(2):
                        if k > 0:
                            pool.wait_ge(ph[k]["nsrc"], 2 * i + q + 1)
                        pool.wait_ge(ph[k]["tp"], 2 * i + q + 1)
                        pool.tensor_copy(stage[:, q, :], source[:, bass.ds(2 * i + q, 1), 0:D].rearrange("p a f -> p (a f)"))\
                            .then_inc(ph[k]["staged"], 1)

            pool.wait_ge(s("loads_x"), 16)
            stage_rows(0, xs)
            pool.wait_ge(s("nb_ready"), 1)
            nb = pool.value_load(plan_i[0:1, NT:NT + 1], min_val=1, max_val=NBMAX)

            def gather(tab, width, stored, win, gath, n0):
                pool.wait_ge(stored, 16)
                with windows(pool, nb) as (i, b, n):
                    for p in range(2):
                        pool.wait_ge(win[p], (n + 1) * 48)
                        pool.nop().then_inc(s("pool_passed"), 1)
                        for c in range(C):
                            pool.indirect_dma_start(
                                out=rows[:, p, c, 0:width], out_offset=None, in_=tab,
                                in_offset=bass.IndirectOffsetOnAxis(ap=srcw[:, p, c:c + 1], axis=0)
                            ).then_inc(gath[p][c // HC], 16)

            gather(table[0], HW, ph[0]["stored"], win, gath, 0)
            for k in range(2):
                stage_rows(k + 1, xs if k == 0 else ys)
                gather(table[k + 1], D, ph[k + 1]["stored"], lay[k]["win"], lay[k]["gath"], k + 1)

        @block.scalar
        def _(act):
            for d_, s_ in ((wfc[:], fc_w), (embr[0:P, 0, :], emb_rel[0:P]), (embr[0:R - P, 1, :], emb_rel[P:R]),
                           (relr[0:P, 0, :], rel_emb[0:P]), (relr[0:R - P, 1, :], rel_emb[P:R]),
                           (wloop[:, 0:D], loop_w), (wr[:, 0, :], W_r[0]), (wr[:, 1, :], W_r[1]),
                           (wself[:, 0, 0:D], W_el[0]), (wself[:, 0, D:2 * D], W_sl[0]),
                           (wself[:, 1, 0:D], W_el[1]), (wself[:, 1, D:2 * D], W_sl[1]),
                           (w2[:], fc2_w.rearrange("a k -> k a"))):
                act.dma_start(d_, s_).then_inc(s("ld_w"), 16)
            act.dma_start(plan2[0:1, 60:61], fc2_w[0:1, 0:1]).then_inc(s("ld_w"), 16)
            act.wait_ge(s("nb_ready"), 1)
            nb = act.value_load(plan_i[0:1, NT:NT + 1], min_val=1, max_val=NBMAX)

            def node_phase(k):
                with act.Fori(0, PAIRS) as i:
                    for q in range(2):
                        act.wait_ge(ph[k]["tp"], 2 * i + q + 3)
                        act.activation(nT[:, q, :], bank[q][:, 0:P], ACT.Copy).then_inc(ph[k]["xt"], 1)

            node_phase(0)
            with windows(act, nb) as (i, b, n):
                for p in range(2):
                    t = 2 * n + p
                    for g in range(NG):
                        w = min(GRP, C - g * GRP)
                        act.wait_ge(s("mx_done"), t * NG + g + 3)
                        act.activation(hotT[:, g * GRP:g * GRP + w, :],
                                       bank[g % 2][:, 0:w * P].rearrange("p (c e) -> p c e", e=P),
                                       ACT.Sign).then_inc(s("mt_done"), 1)
                    act.wait_ge(s("d_ready"), t + 1)
                    act.activation(wexp[:], z[:], ACT.Exp).then_inc(s("w_ready"), 1)
                    act.wait_ge(s("ct_ready"), t + 1)
                    act.activation(cT[:, 0, :], bank[5][:, 0:P], ACT.Copy).then_inc(s("ctc_ready"), 1)
                    act.activation(cT[0:R - P, 1, :], bank[5][0:R - P, P:2 * P], ACT.Copy).then_inc(s("ctc_ready"), 1)
                    act.wait_ge(s("er_ready"), t + 1)
                    act.activation(at(erel, p, i), bank[6][:, 0:D], ACT.Copy).then_inc(s("er_done"), 1)
            for k in range(2):
                if k == 0:
                    act.wait_ge(ph[1]["var"], 2)
                    act.activation(rstd[:], mv[:, :, 1], ACT.Sqrt, bias=epst[:, 0:1]).then_inc(ph[1]["rs"], 1)
                    act.activation(norm[:], degs[:], ACT.Sqrt).then_inc(ph[1]["rs"], 1)
                node_phase(k + 1)
                L = lay[k]
                with windows(act, nb) as (i, b, n):
                    for p in range(2):
                        act.wait_ge(L["sT_ready"], 2 * n + p + 1)
                        act.activation(aggT[:], bank[5][:, 0:P], ACT.Copy).then_inc(L["sTc_ready"], 1)
            act.wait_ge(ph[0]["var"], 1)
            act.activation(rstd[:], mv[:, :, 1], ACT.Sqrt, bias=epst[:, 0:1]).then_inc(ph[0]["rs"], 1)

        @block.tensor
        def _(pe):
            pe.wait_ge(s("consts"), 2)
            pe.wait_ge(s("part_ready"), 1)
            pe.matmul(bank[7][0:1, 0:NT + 2], ones[0:EP, 0:1], part[0:EP, :], start=True, stop=True).then_inc(s("cnt_ps"), 1)
            pe.wait_ge(s("ld_w"), 16 * 14)
            for j in range(3):
                m = pe.matmul(bank[4][:, j:j + 1], wfc[:, j * D:(j + 1) * D], w2[:, 0:1], start=True, stop=True)
            m.then_inc(s("v3_ready"), 1)
            pe.transpose(bank[5][:, 0:P], embr[:, 0, :], ident[:])
            pe.transpose(bank[5][:, P:R], embr[0:R - P, 1, :], ident[0:R - P, 0:R - P]).then_inc(s("emb_t"), 1)
            pe.wait_ge(s("vrb_ready"), 1)
            pe.matmul(bank[6][:, 0:R], vrb[:], embT[:], start=True, stop=True).then_inc(s("rrow_ps"), 1)

            def node_phase(k, rhs, width):
                with pe.Fori(0, PAIRS) as i:
                    for q in range(2):
                        pe.wait_ge(ph[k]["staged"], 2 * i + q + 1)
                        pe.transpose(bank[q][:, 0:P], stage[:, q, :], ident[:]).then_inc(ph[k]["tp"], 1)
                    for q in range(2):
                        pe.wait_ge(ph[k]["xt"], 2 * i + q + 1)
                        pe.wait_ge(ph[k]["nd"], 2 * i + q + 1)
                        pe.matmul(bank[2 + q][:, 0:width], nT[:, q, :], rhs, start=True, stop=True).then_inc(ph[k]["mp"], 1)

            pe.wait_ge(s("vsd"), 1)
            pe.wait_ge(s("loads_x"), 16)
            node_phase(0, wloop[:], D + 2)
            pe.wait_ge(s("lowT"), 1)
            pe.transpose(bank[4][0:1, 0:P], lows[:, 0:1], ident[:]).then_inc(s("low_ps"), 1)
            pe.wait_ge(s("low_in"), 1)
            pe.matmul(bank[4][:, 256:257], ones[0:1, :], lows[0:1, 2:3], start=True, stop=True).then_inc(s("low_ps"), 1)
            pe.wait_ge(s("nb_ready"), 1)
            nb = pe.value_load(plan_i[0:1, NT:NT + 1], min_val=1, max_val=NBMAX)

            with windows(pe, nb) as (i, b, n):
                for p in range(2):
                    t = 2 * n + p
                    for g in range(NG):
                        w = min(GRP, C - g * GRP)
                        pe.wait_ge(s("x_ready"), t * NG + g + 1)
                        pe.wait_ge(s("mx_done"), t * NG + g + 1)
                        pe.wait_ge(s("mt_done"), t * NG + g + 1)
                        for c in range(g * GRP, g * GRP + w):
                            m = pe.transpose(bank[g % 2][:, (c % GRP) * P:(c % GRP + 1) * P], hot[:, c, :], ident[:])
                        m.then_inc(s("xt_ready"), 1)
                    pe.wait_ge(s("bm_ready"), t + 1)
                    pe.wait_ge(s("mt_done"), t * NG + NG + 2)
                    for c in range(C):
                        m = pe.matmul(bank[2][:, 6 * c:6 * c + 6], hotT[:, c, :], bm3[:, :, :], start=True, stop=True)
                    m.then_inc(s("lk_ready"), 1)
                    for c in range(C):
                        if c % HC == 0:
                            pe.wait_ge(s("oh_ready"), 2 * t + c // HC + 1)
                        pe.wait_ge(s("mask_ready"), t * C + c + 1)
                        m = pe.matmul(bank[4][:, 0:R], hotb[:, c, :], toh[:, c, :], start=(c == 0), stop=(c == C - 1))
                    m.then_inc(s("c_ready"), 1)
                    for c in range(C):
                        pe.wait_ge(s("wm_ready"), t * C + c + 1)
                        m = pe.matmul(bank[3][:, 0:D + 2], hot[:, c, :], rows[:, p, c, 0:D + 2], start=(c == 0), stop=(c == C - 1))
                    m.then_inc(s("acc_ready"), 1)
                    pe.wait_ge(s("cc_ready"), t + 1)
                    pe.transpose(bank[5][:, 0:P], cacc[:, p, 0:P], ident[:])
                    pe.transpose(bank[5][0:R - P, P:2 * P], cacc[:, p, P:R], ident[:]).then_inc(s("ct_ready"), 1)
                    pe.wait_ge(s("ctc_ready"), 2 * t + 2)
                    pe.matmul(bank[6][:, 0:D], cT[:, 0, :], relr[:, 0, :], start=True, stop=False)
                    pe.matmul(bank[6][:, 0:D], cT[0:R - P, 1, :], relr[0:R - P, 1, :], start=False, stop=True).then_inc(s("er_ready"), 1)

            for k in range(2):
                node_phase(k + 1, wself[:, k, :], 2 * D)
                L = lay[k]
                with windows(pe, nb) as (i, b, n):
                    for p in range(2):
                        t = 2 * n + p
                        for c in range(C):
                            if c % HC == 0:
                                pe.wait_ge(L["gath"][p][c // HC], (n + 1) * (16 * HC))
                            pe.wait_ge(L["hot_ready"], t * C + c + 1)
                            m = pe.matmul(bank[3 + p][:, 0:D], hot[:, c, :], rows[:, p, c, 0:D], start=(c == 0), stop=(c == C - 1))
                        m.then_inc(L["acc_ready"], 1)
                        pe.wait_ge(L["s_ready"], t + 1)
                        pe.transpose(bank[5][:, 0:P], agg[:], ident[:]).then_inc(L["sT_ready"], 1)
                        pe.wait_ge(L["sTc_ready"], t + 1)
                        pe.matmul(bank[6][:, 0:D], aggT[:], wr[:, k, :], start=True, stop=True).then_inc(L["o_ready"], 1)

        @block.vector
        def _(v):
            ch = Chain(v, s("dve_seq"), s("dve_passed"))
            link, link_alone = ch.link, ch.link_alone
            v.memset(xs[96:P, :, :], 0.0).then_inc(s("xs_zero"), 1)
            v.memset(ones[:], 1.0).then_inc(s("consts"), 1)
            v.memset(epst[:], EPS)
            v.memset(later[:], 1.0)
            v.memset(acc[:], 0.0)
            v.memset(cacc[:], 0.0)
            v.memset(mrun[:], 0.0)
            v.memset(lows[:], 0.0)
            v.memset(cT[:], 0.0)
            link(v.memset(part[:], 0.0))
            v.memset(later[:, 0:1], 0.0)
            v.wait_ge(s("iotas"), 3)
            v.tensor_copy(iota[:], iota_i[:])
            v.tensor_copy(iotab[:], iota_i[:])
            v.tensor_copy(jw[:], jw_i[:])
            link(v.tensor_copy(thr[:], thr_i[:]))

            v.wait_ge(s("ld_dst"), 16)
            smp = scr[0:EP, 0:NS]
            cmp = scr[0:EP, 64:64 + (NT + 1) * NS].rearrange("p (t m) -> p t m", m=NS)
            link(v.tensor_copy(smp, dall[0:EP, 0:EW:SAMP]))
            link(v.tensor_tensor(cmp, scr[0:EP, 0:NS][:, None, :].broadcast_to([EP, NT + 1, NS]),
                                 thr[0:EP, :][:, :, None].broadcast_to([EP, NT + 1, NS]), ALU.is_lt))
            link(v.tensor_reduce(part[0:EP, 0:NT + 1], cmp, AX, ALU.add))
            v.wait_ge(s("ld_next"), 16)
            viol = scr[0:EP, 4096:4096 + EW]
            link(v.tensor_tensor(viol, dall[0:EP, 0:EW], dall[0:EP, EW:2 * EW], ALU.is_gt))
            v.tensor_reduce(part[0:EP, NT + 1:NT + 2], viol, AX, ALU.add).then_inc(s("part_ready"), 1)
            v.wait_ge(s("cnt_ps"), 1)
            cnt, base, need = plan[0:1, 0:NT + 2], plan2[0:1, 0:NT], plan[0:1, 0:NT]
            link(v.tensor_copy(plan[0:1, 0:NT + 2], bank[7][0:1, 0:NT + 2]))
            link(v.tensor_scalar(plan2[0:1, 56:57], plan[0:1, NT + 1:NT + 2], 0.0, None, ALU.is_equal))
            link(v.tensor_scalar(base, plan[0:1, 0:NT], float(SAMP), -float(SAMP), ALU.mult, ALU.add))
            link(v.tensor_scalar(base, base, 0.0, plan2[0:1, 56:57], ALU.max, ALU.mult))
            v.tensor_scalar(plan2[0:1, 57:58], plan2[0:1, 56:57], -2.0 * E, 2.0 * E, ALU.mult, ALU.add)
            link(v.scalar_tensor_tensor(part[0:1, 0:NT], plan[0:1, 1:NT + 1], float(SAMP), base, ALU.mult, ALU.subtract))
            link(v.tensor_reduce(plan2[0:1, 58:59], part[0:1, 0:NT], AX, ALU.max))
            link(v.tensor_tensor(plan2[0:1, 59:60], plan2[0:1, 58:59], plan2[0:1, 57:58], ALU.max))
            link(v.tensor_scalar(part[0:1, 0:NBMAX], jw[0:1, :], plan2[0:1, 59:60], None, ALU.is_lt))
            link(v.tensor_reduce(plan2[0:1, NT:NT + 1], part[0:1, 0:NBMAX], AX, ALU.add))
            v.tensor_copy(plan_i[0:1, 0:NT + 1], plan2[0:1, 0:NT + 1]).then_inc(s("nb_ready"), 1)
            v.wait_ge(s("nb_ready"), 1)
            nb = v.value_load(plan_i[0:1, NT:NT + 1], min_val=1, max_val=NBMAX)

            v.wait_ge(s("v3_ready"), 1)
            link(v.tensor_copy(v3[:], bank[4][:, 0:3]))
            v.wait_ge(s("emb_t"), 1)
            v.tensor_copy(wloop[:, D:D + 2], v3[:, 0:2]).then_inc(s("vsd"), 1)
            link(v.tensor_copy(embT[:], bank[5][:, 0:R]))
            v.tensor_scalar(vrb[:], ones[:], v3[:, 2:3], None, ALU.mult).then_inc(s("vrb_ready"), 1)
            v.wait_ge(s("rrow_ps"), 1)
            link(v.tensor_copy(rrow[:], bank[6][:, 0:R]))
            v.wait_ge(s("loads_x"), 16)
            v.memset(ssd[:], 0.0)
            v.memset(xs[:, :, D + 1:D + 2], 1.0)
            link(v.memset(xs[:, :, D + 2:HW], 0.0))
            for k in range(3):
                v.nop().then_inc(ph[k]["nd"], 2)
            v.nop().then_inc(s("mx_done"), 2)
            v.nop().then_inc(s("mt_done"), 2)
            with v.Fori(0, PAIRS) as i:
                for q in range(2):
                    v.wait_ge(ph[0]["mp"], 2 * i + q + 1)
                    v.tensor_tensor(at(res, q, i), xs[:, bass.ds(2 * i + q, 1), 0:D].rearrange("p a f -> p (a f)"),
                                    bank[2 + q][:, 0:D], ALU.add)
                    v.tensor_copy(at(ssd, q, i), bank[2 + q][:, D:D + 2])
                    v.tensor_copy(xs[:, bass.ds(2 * i + q, 1), D:D + 1].rearrange("p a f -> p (a f)"),
                                  bank[2 + q][:, D:D + 1]).then_inc(ph[0]["nd"], 1)
            v.wait_ge(ph[0]["nd"], NT + 2)
            v.tensor_reduce(lows[:, 0:1], ssd[:, :, 0], AX, ALU.min).then_inc(s("lowT"), 1)
            v.tensor_reduce(lows[0:1, 3:4], rrow[0:1, :], AX, ALU.min)
            v.wait_ge(s("low_ps"), 1)
            link(v.tensor_reduce(lows[0:1, 1:2], bank[4][0:1, 0:P], AX, ALU.min))
            v.tensor_tensor(lows[0:1, 2:3], lows[0:1, 1:2], lows[0:1, 3:4], ALU.add).then_inc(s("low_in"), 1)
            v.wait_ge(s("low_ps"), 2)
            link(v.tensor_copy(low[:, 0:1], bank[4][:, 256:257]))
            link(v.tensor_scalar(low[:, 1:2], low[:, 0:1], -1.0, None, ALU.add))

            LINKS = 2 * L0_LINKS
            with windows(v, nb) as (i, b, n), ch.turns(n, LINKS, nb * PAIRS):
                for p in range(2):
                    t = 2 * n + p
                    v.wait_ge(win[p], (n + 1) * 48)
                    v.tensor_copy(etf[:], etw[:, p, :])
                    link(v.tensor_scalar(dl[:], dstw[:, p, :], thr[:, bass.ds(2 * i + p, 1)], None, ALU.subtract))
                    for c in range(C):
                        r = v.scalar_tensor_tensor(toh[:, c, :], iota[:, 0:R], etf[:, c:c + 1], rrow[:],
                                                   ALU.is_equal, ALU.mult, accum_out=rv[:, c:c + 1])
                    link(r)
                    for j in range(2):
                        v.wait_ge(gath[p][j], (n + 1) * (16 * HC))
                        cs = slice(j * HC, (j + 1) * HC)
                        link(v.tensor_tensor(u[:, cs], rows[:, p, cs, D], rv[:, cs], ALU.add))
                        link(v.tensor_scalar(up[:, cs], u[:, cs], low[:, 0:1], 1.0, ALU.subtract, ALU.add))

                    def reduce_group(g):
                        w = min(GRP, C - g * GRP)
                        v.wait_ge(s("xt_ready"), t * NG + g + 1)
                        return v.tensor_reduce(gmax[:, g:g + 1], bank[g % 2][:, 0:w * P], AX, ALU.max).then_inc(s("mx_done"), 1)

                    for g in range(NG):
                        for c in range(g * GRP, min(C, g * GRP + GRP)):
                            r = v.tensor_scalar(hot[:, c, :], iota[:, 0:P], dl[:, c:c + 1], up[:, c:c + 1],
                                                ALU.is_equal, ALU.mult)
                        r.then_inc(s("x_ready"), 1)
                        if g >= 1:
                            reduce_group(g - 1)
                    reduce_group(NG - 1)
                    v.wait_ge(s("mx_done"), t * NG + NG + 2)
                    bt = ssd[:, bass.ds(2 * i + p, 1), 1:2].rearrange("p a f -> p (a f)")
                    first = later[:, bass.ds(b, 1)]

                    def max_of(o, top):
                        link(v.scalar_tensor_tensor(mold[:, 2:3], top, low[:, 1:2], bt, ALU.add, ALU.add))
                        link(v.scalar_tensor_tensor(o, mold[:, 2:3], 0.01, mold[:, 2:3], ALU.mult, ALU.max))

                    link(v.tensor_reduce(bmax[:], gmax[:], AX, ALU.max))
                    max_of(mold[:, 0:1], mrun[:, p:p + 1])
                    link(v.scalar_tensor_tensor(mrun[:, p:p + 1], mrun[:, p:p + 1], first, bmax[:], ALU.mult, ALU.max))
                    max_of(bm[:, 1:2], mrun[:, p:p + 1])
                    v.nop().then_inc(s("dve_passed"), 1)
                    link(v.tensor_copy(bm[:, 0:1], bt))
                    link(v.tensor_copy(bm3[:, 0, :], bm[:]))
                    link(v.tensor_tensor(bmr[:, 0, :], bm[:], bm3[:, 0, :], ALU.subtract))
                    link(v.tensor_copy(bm3[:, 1, :], bmr[:, 0, :]))
                    link(v.tensor_tensor(bmr[:, 1, :], bmr[:, 0, :], bm3[:, 1, :], ALU.subtract))
                    v.tensor_copy(bm3[:, 2, :], bmr[:, 1, :]).then_inc(s("bm_ready"), 1)
                    v.tensor_tensor(z[:, C:C + 1], mold[:, 0:1], bm[:, 1:2], ALU.subtract)
                    for j in range(2):
                        cs = slice(j * HC, (j + 1) * HC)
                        v.tensor_tensor(toh[:, cs, :], iotab[:, 0:R][:, None, :].broadcast_to([P, HC, R]),
                                        etf[:, cs][:, :, None].broadcast_to([P, HC, R]), ALU.is_equal).then_inc(s("oh_ready"), 1)
                        for c in range(j * HC, (j + 1) * HC):
                            v.tensor_scalar(hotb[:, c, :], iotab[:, 0:P], dl[:, c:c + 1], None, ALU.is_equal).then_inc(s("mask_ready"), 1)
                    v.wait_ge(s("lk_ready"), t + 1)
                    look3 = bank[2][:, 0:6 * C].rearrange("p (c j k) -> p c j k", j=3, k=2)
                    link(v.tensor_copy(look[:], look3[:, :, 0, :]))
                    link(v.tensor_tensor(look[:], look[:], look3[:, :, 1, :], ALU.add))
                    link(v.tensor_tensor(look[:], look[:], look3[:, :, 2, :], ALU.add))
                    link(v.tensor_tensor(z[:, 0:C], u[:], look[:, :, 0], ALU.add))
                    link(v.scalar_tensor_tensor(z2[:], z[:, 0:C], 0.01, z[:, 0:C], ALU.mult, ALU.max))
                    link(v.tensor_tensor(z[:, 0:C], z2[:], look[:, :, 1], ALU.subtract))
                    v.tensor_scalar(z[:], z[:], 1.0, None, ALU.min).then_inc(s("d_ready"), 1)
                    v.wait_ge(s("w_ready"), t + 1)
                    for c in range(C):
                        v.tensor_scalar(hot[:, c, :], iota[:, 0:P], dl[:, c:c + 1], wexp[:, c:c + 1],
                                        ALU.is_equal, ALU.mult).then_inc(s("wm_ready"), 1)
                    v.wait_ge(s("c_ready"), t + 1)
                    v.scalar_tensor_tensor(cacc[:, p, :], cacc[:, p, :], first, bank[4][:, 0:R], ALU.mult, ALU.add).then_inc(s("cc_ready"), 1)
                    v.wait_ge(s("acc_ready"), t + 1)
                    v.nop().then_inc(win_free[p], 1)
                    link(v.tensor_tensor(fin[:, 0:1], wexp[:, C:C + 1], first, ALU.mult))
                    link(v.scalar_tensor_tensor(acc[:, p, 0:D + 2], acc[:, p, 0:D + 2], fin[:, 0:1], bank[3][:, 0:D + 2], ALU.mult, ALU.add))
                    deg, has, no, den, rec = (fin[:, j:j + 1] for j in range(1, 6))
                    link(v.tensor_reduce(deg, cacc[:, p, :], AX, ALU.add))
                    v.tensor_scalar(has, deg, 0.0, None, ALU.is_gt)
                    link(v.tensor_scalar(no, deg, 0.0, None, ALU.is_equal))
                    one = lambda a: a[:, bass.ds(2 * i + p, 1)]
                    v.tensor_scalar(one(degs), deg, 1.0, None, ALU.max)
                    v.tensor_copy(one(niso), has)
                    v.tensor_copy(one(iso), no)
                    link(v.tensor_tensor(den, acc[:, p, D + 1:D + 2], no, ALU.add))
                    link(v.reciprocal(rec, den))
                    link(v.tensor_tensor(rec, rec, has, ALU.mult))
                    link(v.scalar_tensor_tensor(agg[:], acc[:, p, 0:D], rec, at(res, p, i), ALU.mult, ALU.add))
                    link_alone(v.scalar_tensor_tensor(agg[:], xs[:, bass.ds(2 * i + p, 1), 0:D].rearrange("p a f -> p (a f)"), no, agg[:],
                                                ALU.mult, ALU.add))
                    v.tensor_copy(at(ys, p, i), agg[:])
                    link_alone(v.bn_stats(stat[:], agg[:]))
                    link_alone(v.bn_aggr(fin[:, 6:8], stat[:]))
                    link_alone(v.tensor_copy(at(mv, p, i), fin[:, 6:8]))
            v.nop().then_inc(ph[1]["var"], 2)

            def layer_norm(k, to):
                v.wait_ge(ph[k]["rs"], 2 if k == 1 else 1)
                if k == 1:
                    v.reciprocal(norm[:], norm[:])
                link_alone(v.reciprocal(rstd[:], rstd[:]))
                with v.Fori(0, PAIRS) as i:
                    for q in range(2):
                        tl = bass.ds(2 * i + q, 1)
                        v.tensor_scalar(to[:, tl, 0:D].rearrange("p a f -> p (a f)"), at(ys, q, i),
                                        mv[:, tl, 0:1].rearrange("p a f -> p (a f)"), rstd[:, tl],
                                        ALU.subtract, ALU.mult).then_inc(ph[k]["nsrc"], 1)

            layer_norm(1, xs)
            for k in range(2):
                with v.Fori(0, PAIRS) as i, ch.turns(i, 2, PAIRS):
                    for q in range(2):
                        tl = bass.ds(2 * i + q, 1)
                        v.wait_ge(ph[k + 1]["mp"], 2 * i + q + 1)
                        link(v.tensor_scalar(tmp[:, q, :], bank[2 + q][:, D:2 * D], niso[:, tl], None, ALU.mult))
                        v.scalar_tensor_tensor(at(res, q, i), bank[2 + q][:, 0:D], iso[:, tl], tmp[:, q, :],
                                               ALU.mult, ALU.add).then_inc(ph[k + 1]["nd"], 1)
                v.wait_ge(ph[k + 1]["nd"], NT + 2)
                L = lay[k]
                with windows(v, nb) as (i, b, n), ch.turns(n, 2 * (6 + 3 * k), nb * PAIRS):
                    for p in range(2):
                        t = 2 * n + p
                        tl = bass.ds(2 * i + p, 1)
                        v.wait_ge(L["win"][p], (n + 1) * 48)
                        link(v.tensor_scalar(dl[:], dstw[:, p, :], thr[:, tl], None, ALU.subtract))
                        for c in range(C):
                            v.tensor_scalar(hot[:, c, :], iota[:, 0:P], dl[:, c:c + 1], None, ALU.is_equal).then_inc(L["hot_ready"], 1)
                        v.wait_ge(L["acc_ready"], t + 1)
                        link(v.scalar_tensor_tensor(acc[:, p, 0:D], acc[:, p, 0:D], later[:, bass.ds(b, 1)], bank[3 + p][:, 0:D],
                                                    ALU.mult, ALU.add))
                        v.nop().then_inc(L["win_free"][p], 1)
                        link(v.tensor_tensor(agg[:], acc[:, p, 0:D], at(erel, p, i), ALU.add))
                        v.nop().then_inc(L["s_ready"], 1)
                        v.wait_ge(L["o_ready"], t + 1)
                        link(v.scalar_tensor_tensor(tmp[:, 0, :], bank[6][:, 0:D], norm[:, tl], at(res, p, i), ALU.mult, ALU.add))
                        link_alone(v.scalar_tensor_tensor(tmp[:, 1, :], tmp[:, 0, :], SLOPE, tmp[:, 0, :], ALU.mult, ALU.max))
                        if k == 0:
                            link_alone(v.tensor_copy(at(ys, p, i), tmp[:, 1, :]))
                        else:
                            link_alone(v.tensor_tensor(agg[:], xs[:, tl, 0:D].rearrange("p a f -> p (a f)"), tmp[:, 1, :], ALU.add))
                            v.tensor_copy(at(ys, p, i), agg[:])
                            link_alone(v.bn_stats(stat[:], agg[:]))
                            link_alone(v.bn_aggr(fin[:, 6:8], stat[:]))
                            link_alone(v.tensor_copy(at(mv, p, i), fin[:, 6:8]))
                if k == 0:
                    v.nop().then_inc(ph[2]["nsrc"], NT)
            v.nop().then_inc(ph[0]["var"], 1)
            layer_norm(0, ys)
            v.wait_ge(ph[0]["nsrc"], NT)
            v.nop().then_inc(s("st_out"), 1)


_INS = ['x', 'src', 'dst', 'edge_type_200', 'L0_gnn_emb_rel', 'L0_gnn_loop_weight', 'L0_gnn_attn_fc_w', 'L0_gnn_attn_fc2_w',
        'L1_gnn_rel_embed', 'L1_gnn_W_r1', 'L1_gnn_W_sl1', 'L1_gnn_W_el1', 'L1_gnn_W_r2', 'L1_gnn_W_sl2', 'L1_gnn_W_el2']


def kernel(**inputs):
    import numpy as _np
    import concourse.bacc as _bacc
    from concourse import mybir as _mybir
    from concourse.bass_utils import run_bass_kernel_spmd as _run

    nc = _bacc.Bacc("TRN2", target_bir_lowering=False, num_devices=1)
    arrays, a = {}, {}
    for name in _INS:
        v = _np.ascontiguousarray(inputs[name])
        arrays[f"in_{name}_dram"] = v
        a[name] = nc.dram_tensor(f"in_{name}_dram", v.shape, _mybir.dt.from_np(v.dtype), kind="ExternalInput").ap()
    out = nc.dram_tensor("out_0_dram", (N, D), F32, kind="ExternalOutput").ap()
    build(nc, a['x'], a['src'], a['dst'], a['edge_type_200'], a['L0_gnn_emb_rel'], a['L0_gnn_loop_weight'],
          a['L0_gnn_attn_fc_w'], a['L0_gnn_attn_fc2_w'], a['L1_gnn_rel_embed'],
          [a['L1_gnn_W_r1'], a['L1_gnn_W_r2']], [a['L1_gnn_W_sl1'], a['L1_gnn_W_sl2']],
          [a['L1_gnn_W_el1'], a['L1_gnn_W_el2']], out)
    r = _run(nc, [arrays], core_ids=[0])
    return r.results[0]["out_0_dram"]
```

```python
from contextlib import ExitStack, contextmanager

import concourse.bass as bass
from concourse import mybir

F32 = mybir.dt.float32
BF16 = mybir.dt.bfloat16
I32 = mybir.dt.int32
ALU = mybir.AluOpType
ACT = mybir.ActivationFunctionType
AX = mybir.AxisListType.X

P = 128
N, D, R, E = 6250, 128, 200, 200000
TN = 125
NT = N // TN
PAIRS = NT // 2
C = 34
HC = C // 2
WIN = C * P
SAMP = 32
EP = 125
EW = E // EP
NS = EW // SAMP
NBMAX = -(-E // WIN)
PADW = -(-(NBMAX * WIN + WIN) // P)
PAD = P * PADW
NODST = 16383.0
HW = 132
GRP = 4
NG = -(-C // GRP)
TGRP = 8
NTG = -(-C // TGRP)
L0_LINKS = 37
G = 5
KG = N // G
GB = 128
NGB = -(-KG // GB)
KGP = NGB * GB
GC = 2
GRAN = SAMP
GW = GC * P // GRAN
ROWP = 32
BG = 50
BD = BG * G
NB = KG // BG
HI = NT
CW = G * HI
RG = 5
NAB = 5
LEAD = 2
SLOPE = (1.0 / 8.0 + 1.0 / 3.0) / 2.0
EPS = 1e-5
assert NB * BG == KG and KG * G == N and BD == 2 * TN and (BG // 2) % NAB == 0 and 2 * CW <= 512 and CW <= 256
assert EP * EW == E and NS * SAMP == EW and NT * TN == N and PAIRS * 2 == NT


class Chain:

    def __init__(self, eng, sem, passed):
        self.passed = passed
        self.eng, self.sem, self.base, self.count = eng, sem, 0, 0

    def link(self, ins):
        ins.then_inc(self.sem, 1)
        self.count += 1
        self.eng.wait_ge(self.sem, self.base + self.count)

    def link_alone(self, ins):
        self.link(ins)
        self.eng.nop().then_inc(self.passed, 1)

    @contextmanager
    def turns(self, turn, each, turns):
        outer = self.base + self.count
        self.base, self.count = outer + turn * each, 0
        yield
        assert self.count == each, (self.count, each)
        self.base, self.count = outer + turns * each, 0


def build(nc, x, src, dst, etype, emb_rel, loop_w, fc_w, fc2_w, rel_emb, W_r, W_sl, W_el, out):
    ctx = ExitStack()
    with ctx:
        def sb(name, shape, dt=F32):
            return ctx.enter_context(nc.sbuf_tensor(name, shape, dt))

        def sem(name):
            return ctx.enter_context(nc.semaphore(name))

        def dram(name, shape, dt):
            return nc.dram_tensor(name, shape, dt, kind="Internal").ap()

        srcp, dstp, etp = (dram(n, (E + PAD,), I32) for n in ("src_padded", "dst_padded", "etype_padded"))
        rec = dram("edge_records", (E // GRAN + ROWP, 2 * GRAN), F32)
        starts = dram("group_starts", (KGP + NGB,), F32)
        counts = dram("counts", (NB, TN, HI * BD), BF16)
        table = [dram("rows0", (N, HW), F32), dram("rows1", (N, D), F32), dram("rows2", (N, D), F32)]

        arena = sb("arena", [P, 27680])
        arena_at = [0]

        def carve(shape, dt=F32):
            n = 1
            for d_ in shape[1:]:
                n *= d_
            n = n if dt in (F32, I32) else n // 2
            v_ = arena[:, arena_at[0]:arena_at[0] + n]
            arena_at[0] += n
            assert arena_at[0] <= 27680
            if dt != F32:
                v_ = v_.bitcast(dt)
            names = "abcd"[:len(shape) - 1]
            if len(names) > 1:
                v_ = v_.rearrange("p (%s) -> p %s" % (" ".join(names), " ".join(names)), **dict(zip(names[1:], shape[2:])))
            return v_

        res = sb("res", [P, NT, D])
        ys = sb("ys", [P, NT, D])
        erT = sb("erT", [P, N])
        degt = sb("degt", [P, NT])
        ssd = sb("ssd", [P, NT, 2])
        mv = sb("mv", [P, NT, 2])
        rstd = sb("rstd", [P, NT])
        degs = sb("degs", [P, NT])
        norm = sb("norm", [P, NT])
        iso = sb("iso", [P, NT])
        niso = sb("niso", [P, NT])
        rows = carve([P, 2, C, HW])
        srcw = sb("srcw", [P, 2, C], I32)
        dstw = sb("dstw", [P, 2, C], I32)
        etw = sb("etw", [P, 2, C], I32)
        etf = sb("etf", [P, C])
        dl = sb("dl", [P, C])
        rv = sb("rv", [P, C])
        u = sb("u", [P, C])
        up = sb("up", [P, P])
        upT = sb("upT", [C, P])
        junk = sb("junk", [P, 2, R], BF16)
        identb = sb("identb", [P, P], BF16)
        z = sb("z", [P, C + 1])
        z2 = sb("z2", [P, C])
        wexp = sb("wexp", [P, C + 1])
        hot = carve([P, C, P])
        hotb = carve([P, C, P], BF16)
        hotT = carve([P, C, P], BF16)
        toh = carve([P, C, R], BF16)
        xs = carve([P, NT, HW])
        arena_at[0] = 0
        AT = carve([P, 2, HI, BD], BF16)
        hs = carve([P, 3, NT, D], BF16)
        ohm = carve([P, RG, GC, CW], BF16)
        ohl = carve([P, RG, GC, P], BF16)
        idx = carve([P, 2 * GC, KGP], BF16)
        idxf = carve([P, 2, 2 * GC, BG])
        x1r = carve([P, 2, 2, D])
        arena_at[0] = 0
        recw = carve([P, NGB, GW, 2 * GRAN])
        recc = carve([P, 2, 2, GW * GRAN])
        rem = ohm[:, 0:3, :, :].rearrange("p a b c -> p (a b c)")[:, 0:10 * D].bitcast(F32).rearrange("p (a b) -> p a b", b=D)
        gmax = sb("gmax", [P, NG])
        bmax = sb("bmax", [P, 1])
        mrun = sb("mrun", [P, 2])
        mold = sb("mold", [P, 4])
        bm = sb("bm", [P, 2])
        bmr = sb("bmr", [P, 2, 2])
        bm3 = sb("bm3", [P, 3, 2], BF16)
        look = sb("look", [P, C, 2])
        acc = sb("acc", [P, 2, HW])
        cacc = sb("cacc", [P, 2, R])
        sT = sb("sT", [P, BD])
        gst_i = sb("gst_i", [P, 2, NGB], I32)
        gstf = sb("gstf", [P, 2, NGB])
        gidx = sb("gidx", [P, GW, NGB], I32)
        kcol = sb("kcol", [P, NGB])
        tri = sb("tri", [P, P])
        ok_i = sb("ok_i", [1, 1], I32)
        cT = sb("cT", [P, 2, P])
        fin = sb("fin", [P, 8])
        stat = sb("stat", [P, 6])
        agg = sb("agg", [P, D])
        tmp = sb("tmp", [P, 2, D])
        stage = sb("stage", [P, 2, D])
        nT = sb("nT", [P, 2, P])
        iota = sb("iota", [P, 256])
        iotab = sb("iotab", [P, 256], BF16)
        thr_i = sb("thr_i", [P, NT + 1], I32)
        thr = sb("thr", [P, NT + 1])
        jw_i = sb("jw_i", [P, NBMAX], I32)
        jw = sb("jw", [P, NBMAX])
        later = sb("later", [P, NBMAX])
        ident = sb("ident", [P, P])
        ones = sb("ones", [P, P])
        w2 = sb("w2", [P, 1])
        v3 = sb("v3", [P, 3])
        rrow = sb("rrow", [P, R])
        relr = sb("relr", [P, 2, D])
        wr = sb("wr", [P, 2, D])
        wself = sb("wself", [P, 2, 2 * D])
        epst = sb("epst", [P, 1])
        plan = sb("plan", [P, 64])
        plan2 = sb("plan2", [P, 64])
        plan_i = sb("plan_i", [1, 64], I32)
        part = sb("part", [P, NT + 2])
        lows = sb("lows", [P, 4])
        low = sb("low", [P, 2])
        padz = hot[:, :, :].rearrange("p a b -> p (a b)").bitcast(I32)
        iota_i = hotT[:, 0:4, :].rearrange("p a b -> p (a b)").bitcast(I32)
        kcol_i = hotT[:, 4:8, :].rearrange("p a b -> p (a b)").bitcast(I32)[:, 0:NGB]
        padr = hotT[:, 8:12, :].rearrange("p a b -> p (a b)").bitcast(F32)[:, 0:2 * GRAN]
        recs = toh[:, 0:32, :].rearrange("p a b -> p (a b)").bitcast(F32)[:, 0:EW * 2].rearrange("p (j r) -> p j r", r=2 * GRAN)
        hotf = hot[:, :, :].rearrange("p a b -> p (a b)")
        early = hotb[:, :, :].rearrange("p a b -> p (a b)").bitcast(F32)
        wfc, vrb, embT, wloop = early[:, 0:384], early[:, 384:512], early[:, 512:712], early[:, 712:842]
        embr = early[:, 842:1098].rearrange("p (a f) -> p a f", a=2)
        scr = rows[:, :, :, :].rearrange("p s a b -> p (s a b)")
        dall = scr[:, 5696:5696 + 2 * EW].bitcast(I32)

        bank = [ctx.enter_context(nc.psum_tensor(f"bank{i}", [P, 512], F32)) for i in range(8)]

        S = {}

        def s(name):
            if name not in S:
                S[name] = sem(name)
            return S[name]

        for name in ("up_ready u_ready tr_ready upT_ps upT_ready rv_done recs_ready rec_stored padr_ready ld_src deg_ready pre_ps rp_ready rpT rpT_ready gst_stored st_pad "
                     "gst_loaded gi_ready wT_ready wT_ps idx_done ok_ps ok_ready tri_ready ld_w loads_x ld_dst ld_next "
                     "out_stored pads edges iotas consts nb_ready v3_ready vrb_ready vsd emb_t rrow_ps part_ready cnt_ps "
                     "lowT low_ps low_in dve_seq dve_passed pool_passed act_passed pool_c mx_done mt_done "
                     "bm_ready lk_ready d_ready w_ready mask_ready wm_ready acc_ready c_ready cc_ready ct_ready "
                     "ctc_ready er_ready er_done st_out sp_passed ").split():
            s(name)
        win = [sem(f"win{p}") for p in range(2)]
        win_free = [sem(f"win_free{p}") for p in range(2)]
        gath = [[sem(f"gath{p}{j}") for j in range(2)] for p in range(2)]
        at_stored = [sem(f"at_stored{q}") for q in range(2)]
        at_loaded = [sem(f"at_loaded{q}") for q in range(2)]
        wgat = [sem(f"wgat{b}") for b in range(NGB)]
        dense = [{n: sem(f"{n}_d{k}") for n in ("oh", "built", "ev", "dn", "st", "ou", "split", "x1_free", "seq")}
                 | {"x1": [sem(f"x1_d{k}{q}") for q in range(2)]} for k in range(2)]
        lay = [{"hot_ready": dense[k]["oh"], "acc_ready": dense[k]["dn"], "s_ready": dense[k]["st"], "sT_ready": dense[k]["built"],
                "sTc_ready": dense[k]["ev"], "o_ready": dense[k]["ou"],
                "win": [sem(f"win_{k}{p}") for p in range(2)],
                "win_free": [sem(f"win_free_{k}{p}") for p in range(2)],
                "gath": [[sem(f"gath_{k}{p}{j}") for j in range(2)] for p in range(2)]} for k in range(2)]
        ph = [{n: sem(f"{n}_ph{k}") for n in ("nsrc", "staged", "tp", "xt", "mp", "nd", "stored")
               + (("var", "rs") if k < 2 else ())} for k in range(3)]

        block = ctx.enter_context(nc.Block())

        def windows(eng, nb):
            @contextmanager
            def loop():
                with eng.Fori(0, PAIRS) as i:
                    with eng.Fori(0, nb) as b:
                        yield i, b, i * nb + b
            return loop()

        def at(t, q, i):
            return t[:, bass.ds(2 * i + q, 1), :].rearrange("p a f -> p (a f)")

        def window_list(a, start):
            return a[bass.ds(start, WIN)].rearrange("(p c) -> p c", c=C)

        @block.sync
        def _(sp):
            sp.dma_start(dall[0:EP, 0:EW], dst.rearrange("(p e) -> p e", p=EP)).then_inc(s("ld_dst"), 16)
            sp.wait_ge(s("xs_zero"), 1)
            sp.dma_start(xs[0:TN, :, 0:D], x.rearrange("(t p) f -> p t f", p=TN)).then_inc(s("loads_x"), 16)
            for a, b in ((src, srcp), (dst, dstp), (etype, etp)):
                sp.dma_start(b[0:E].rearrange("(p e) -> p e", p=EP), a.rearrange("(p e) -> p e", p=EP)).then_inc(s("edges"), 16)
            sp.wait_ge(s("pads"), 1)
            sp.dma_start(srcp[E:E + PAD].rearrange("(p e) -> p e", p=P), padz[:, 0:PADW]).then_inc(s("edges"), 16)
            sp.dma_start(etp[E:E + PAD].rearrange("(p e) -> p e", p=P), padz[:, 0:PADW]).then_inc(s("edges"), 16)
            sp.wait_ge(s("pads"), 2)
            sp.dma_start(dstp[E:E + PAD].rearrange("(p e) -> p e", p=P), padz[:, PADW:2 * PADW]).then_inc(s("edges"), 16)
            sp.wait_ge(s("edges"), 96)
            sp.dma_start(dall[0:EP, EW:2 * EW], dstp[1:E + 1].rearrange("(p e) -> p e", p=EP)).then_inc(s("ld_next"), 16)
            sp.dma_start(ys[0:EP, :, :].rearrange("p a b -> p (a b)").bitcast(I32)[:, 0:EW], src.rearrange("(p e) -> p e", p=EP))\
                .then_inc(s("ld_src"), 16)
            sp.wait_ge(s("padr_ready"), 1)
            sp.dma_start(rec[E // GRAN:E // GRAN + ROWP], padr[0:ROWP, :]).then_inc(s("rec_stored"), 16)
            sp.wait_ge(s("recs_ready"), 1)
            sp.dma_start(rec[0:E // GRAN].rearrange("(p j) r -> p j r", p=EP), recs[0:EP]).then_inc(s("rec_stored"), 16)
            sp.wait_ge(ph[0]["nd"], NT + 2)
            sp.dma_start(table[0].rearrange("(t p) f -> p t f", p=TN), xs[0:TN, :, :]).then_inc(ph[0]["stored"], 16)
            sp.wait_ge(s("nb_ready"), 1)
            nb = sp.value_load(plan_i[0:1, NT:NT + 1], min_val=1, max_val=NBMAX)

            def load_windows(win, free, x1=False):
                with windows(sp, nb) as (i, b, n):
                    for p in range(2):
                        first = sp.value_load(plan_i[0:1, bass.ds(2 * i + p, 1)], min_val=0, max_val=E)
                        sp.wait_ge(free[p], n + 1)
                        for a, w in ((srcp, srcw), (dstp, dstw), (etp, etw)):
                            sp.dma_start(w[:, p, :], window_list(a, first + b * WIN)).then_inc(win[p], 16)
                        if x1:
                            sp.dma_start(x1r[0:TN, p, 0, :], table[1][bass.ds((2 * i + p) * TN, TN)]).then_inc(win[p], 16)

            load_windows(win, win_free)
            sp.wait_ge(win_free[0], nb * PAIRS + 1)
            for a, w in ((srcp, srcw), (dstp, dstw), (etp, etw)):
                sp.dma_start(w[:, 0, :], window_list(a, 0)).then_inc(win[0], 16)
            sp.wait_ge(s("st_pad"), 1)
            sp.dma_start(starts[KG:KGP + NGB].rearrange("(a n) -> a n", a=1), part[0:1, 0:KGP + NGB - KG]).then_inc(s("gst_stored"), 16)
            sp.wait_ge(s("rpT_ready"), 1)
            sp.dma_start(starts[0:KG].rearrange("(t g) -> t g", g=TN // G), sT[0:NT, 0:TN // G]).then_inc(s("gst_stored"), 16)
            sp.wait_ge(s("gst_stored"), 32)
            for j in range(2):
                sp.dma_start(gstf[:, j, :], starts[j:j + KGP].rearrange("(b p) -> p b", p=GB),
                             allow_slow_non_contiguous=True).then_inc(s("gst_loaded"), 16)
            sp.wait_ge(s("ok_ready"), 1)
            ok = sp.value_load(ok_i[0:1, 0:1], min_val=0, max_val=1)
            for k in range(2):
                sp.wait_ge(ph[k + 1]["nsrc"], NT)
                sp.dma_start(table[k + 1].rearrange("(t p) f -> p t f", p=TN), ys[0:TN, :, :]).then_inc(ph[k + 1]["stored"], 16)
                if k == 1:
                    sp.wait_ge(ph[1]["stored"], 16)
                    with sp.If(ok):
                        sp.wait_ge(dense[0]["dn"], NB + 2)
                        for q in range(2):
                            sp.wait_ge(at_stored[q], 16 * ((NB + 1 - q) // 2 + 1))

                        def load_block(B, q, n):
                            sp.wait_ge(dense[1]["dn"], n + 1)
                            sp.dma_start(AT[0:TN, q, :, :].rearrange("p h d -> p (h d)"),
                                         counts[bass.ds(B, 1)].rearrange("a p c -> (a p) c")).then_inc(at_loaded[q], 16)
                            sp.wait_ge(dense[1]["x1_free"], n + 1)
                            sp.dma_start(x1r[0:TN, q, :, :], table[1][bass.ds(B * BD, BD)].rearrange("(h p) f -> p h f", p=TN))\
                                .then_inc(dense[1]["x1"][q], 16)
                        with sp.Fori(0, NB // 2) as i:
                            for q in range(2):
                                load_block(2 * i + q, q, 2 * i + q)
                        load_block(NB - 1, 0, NB - 1)
                    with sp.Else():
                        load_windows(lay[k]["win"], lay[k]["win_free"], True)
                else:
                    with sp.If(ok):
                        def store_counts(B, q):
                            sp.wait_ge(dense[0]["ev"], (B + 1) * (BG // 2) + NAB)
                            sp.dma_start(counts[bass.ds(B, 1)].rearrange("a p c -> (a p) c"),
                                         AT[0:TN, q, :, :].rearrange("p h d -> p (h d)")).then_inc(at_stored[q], 16)
                        with sp.Fori(0, NB // 2) as i:
                            for q in range(2):
                                store_counts(2 * i + q, q)
                        store_counts(NB - 1, 0)
                    with sp.Else():
                        load_windows(lay[k]["win"], lay[k]["win_free"])
            sp.wait_ge(s("st_out"), 1)
            sp.dma_start(out.rearrange("(t p) f -> p t f", p=TN), ys[0:TN, :, :]).then_inc(s("out_stored"), 16)
            sp.wait_ge(s("out_stored"), 16)

        @block.gpsimd
        def _(pool):
            pool.memset(padz[:, 0:PADW], 0).then_inc(s("pads"), 1)
            pool.memset(padz[:, PADW:2 * PADW], int(NODST)).then_inc(s("pads"), 1)
            pool.iota(iota_i[:], [[1, 256]], base=0, channel_multiplier=0).then_inc(s("iotas"), 1)
            pool.iota(thr_i[:], [[TN, NT + 1]], base=0, channel_multiplier=0).then_inc(s("iotas"), 1)
            pool.iota(kcol_i[:], [[CW * GB, NGB]], base=0, channel_multiplier=CW).then_inc(s("iotas"), 1)
            pool.iota(jw_i[:], [[WIN, NBMAX]], base=0, channel_multiplier=0).then_inc(s("iotas"), 1)
            pool.memset(ident[:], 0.0).then_inc(s("pool_c"), 1)
            pool.wait_ge(s("pool_c"), 1)
            pool.affine_select(out=ident[:], in_=ident[:], compare_op=ALU.not_equal, fill=1.0, base=0,
                               pattern=[[-1, P]], channel_multiplier=1).then_inc(s("consts"), 1)
            pool.memset(tri[:], 0.0).then_inc(s("pool_c"), 1)
            pool.wait_ge(s("pool_c"), 2)
            pool.affine_select(out=tri[:], in_=tri[:], compare_op=ALU.is_ge, fill=1.0, base=0,
                               pattern=[[-1, P]], channel_multiplier=1).then_inc(s("tri_ready"), 1)
            pool.memset(padr[:], -1000.0).then_inc(s("padr_ready"), 1)
            for p in range(2):
                pool.nop().then_inc(win_free[p], 1)
                for k in range(2):
                    pool.nop().then_inc(lay[k]["win_free"][p], 1)
            for k in range(3):
                pool.nop().then_inc(ph[k]["tp"], 2)

            def stage_rows(k, source):
                with pool.Fori(0, PAIRS) as i:
                    for q in range(2):
                        if k > 0:
                            pool.wait_ge(ph[k]["nsrc"], 2 * i + q + 1)
                        pool.wait_ge(ph[k]["tp"], 2 * i + q + 1)
                        pool.tensor_copy(stage[:, q, :], source[:, bass.ds(2 * i + q, 1), 0:D].rearrange("p a f -> p (a f)"))\
                            .then_inc(ph[k]["staged"], 1)

            pool.wait_ge(s("loads_x"), 16)
            stage_rows(0, xs)
            pool.wait_ge(s("nb_ready"), 1)
            nb = pool.value_load(plan_i[0:1, NT:NT + 1], min_val=1, max_val=NBMAX)

            def gather(tab, width, stored, win, gath, n0, lists=48):
                pool.wait_ge(stored, 16)
                with windows(pool, nb) as (i, b, n):
                    for p in range(2):
                        pool.wait_ge(win[p], (n + 1) * lists)
                        pool.nop().then_inc(s("pool_passed"), 1)
                        for c in range(C):
                            pool.indirect_dma_start(
                                out=rows[:, p, c, 0:width], out_offset=None, in_=tab,
                                in_offset=bass.IndirectOffsetOnAxis(ap=srcw[:, p, c:c + 1], axis=0)
                            ).then_inc(gath[p][c // HC], 16)

            gather(table[0], HW, ph[0]["stored"], win, gath, 0)
            pool.wait_ge(s("rec_stored"), 32)
            pool.wait_ge(s("gi_ready"), 1)
            for b in range(NGB):
                for j in range(GW):
                    pool.indirect_dma_start(
                        out=recw[:, b, j, :], out_offset=None, in_=rec,
                        in_offset=bass.IndirectOffsetOnAxis(ap=gidx[:, j, b:b + 1], axis=0)).then_inc(wgat[b], 16)
            pool.wait_ge(s("ok_ready"), 1)
            ok = pool.value_load(ok_i[0:1, 0:1], min_val=0, max_val=1)
            for k in range(2):
                with pool.If(ok):
                    pool.nop().then_inc(s("pool_passed"), 1)
                with pool.Else():
                    gather(table[k + 1], D, ph[k + 1]["stored"], lay[k]["win"], lay[k]["gath"], k + 1, 48 + 16 * k)

        @block.scalar
        def _(act):
            for d_, s_ in ((wfc[:], fc_w), (embr[0:P, 0, :], emb_rel[0:P]), (embr[0:R - P, 1, :], emb_rel[P:R]),
                           (relr[0:P, 0, :], rel_emb[0:P]), (relr[0:R - P, 1, :], rel_emb[P:R]),
                           (wloop[:, 0:D], loop_w), (wr[:, 0, :], W_r[0]), (wr[:, 1, :], W_r[1]),
                           (wself[:, 0, 0:D], W_el[0]), (wself[:, 0, D:2 * D], W_sl[0]),
                           (wself[:, 1, 0:D], W_el[1]), (wself[:, 1, D:2 * D], W_sl[1]),
                           (w2[:], fc2_w.rearrange("a k -> k a"))):
                act.dma_start(d_, s_).then_inc(s("ld_w"), 16)
            act.dma_start(plan2[0:1, 60:61], fc2_w[0:1, 0:1]).then_inc(s("ld_w"), 16)
            act.wait_ge(s("nb_ready"), 1)
            nb = act.value_load(plan_i[0:1, NT:NT + 1], min_val=1, max_val=NBMAX)

            def node_phase(k):
                with act.Fori(0, PAIRS) as i:
                    if k > 0:
                        for q in range(2):
                            act.wait_ge(ph[k]["nsrc"], 2 * i + q + 1)
                            act.wait_ge(ph[k]["tp"], 2 * i + q + 1)
                            act.activation(stage[:, q, :], at(ys, q, i), ACT.Copy).then_inc(ph[k]["staged"], 1)
                    for q in range(2):
                        act.wait_ge(ph[k]["tp"], 2 * i + q + 3)
                        act.activation(nT[:, q, :], bank[q][:, 0:P], ACT.Copy).then_inc(ph[k]["xt"], 1)

            node_phase(0)
            with windows(act, nb) as (i, b, n):
                for p in range(2):
                    t = 2 * n + p
                    for g in range(NTG):
                        w = min(TGRP, C - g * TGRP)
                        act.wait_ge(s("tr_ready"), t * NTG + g + 1)
                        act.activation(hotT[:, g * TGRP:g * TGRP + w, :],
                                       bank[g % 2][:, :].bitcast(BF16)[:, 0:w * P].rearrange("p (c e) -> p c e", e=P),
                                       ACT.Copy).then_inc(s("mt_done"), 1)
                    act.wait_ge(s("d_ready"), t + 1)
                    act.activation(wexp[:], z[:], ACT.Exp).then_inc(s("w_ready"), 1)
                    act.wait_ge(s("w_ready"), t + 1)
                    for c in range(C):
                        act.activation(hot[:, c, :], hotb[:, c, :], ACT.Copy, scale=wexp[:, c:c + 1]).then_inc(s("wm_ready"), 1)
                    act.wait_ge(s("ct_ready"), t + 1)
                    act.activation(cT[:, 0, :], bank[5][:, 0:P], ACT.Copy).then_inc(s("ctc_ready"), 1)
                    act.activation(cT[0:R - P, 1, :], bank[5][0:R - P, P:2 * P], ACT.Copy).then_inc(s("ctc_ready"), 1)
                    act.wait_ge(s("er_ready"), t + 1)
                    act.activation(erT[:, bass.ds((2 * i + p) * TN, TN)], bank[5][:, 2 * P:2 * P + TN], ACT.Copy).then_inc(s("er_done"), 1)
            act.wait_ge(ph[1]["var"], 2)
            act.activation(rstd[:], mv[:, :, 1], ACT.Sqrt, bias=epst[:, 0:1]).then_inc(ph[1]["rs"], 1)
            act.activation(norm[:], degs[:], ACT.Sqrt).then_inc(ph[1]["rs"], 1)
            node_phase(1)
            for b in range(NGB):
                act.wait_ge(s("wT_ps"), b + 1)
                act.activation(idx[:, :, b * GB:(b + 1) * GB], bank[4 + b % 2][:, :].rearrange("p (m g) -> p m g", g=GB), ACT.Copy)\
                    .then_inc(s("idx_done"), 1)
            act.wait_ge(s("ok_ready"), 1)
            ok = act.value_load(ok_i[0:1, 0:1], min_val=0, max_val=1)
            for k in range(2):
                if k == 1:
                    node_phase(2)
                with act.If(ok):
                    X = dense[k]

                    def block(B, q, half):
                        act.wait_ge(X["dn"], B + 1)
                        act.wait_ge(at_stored[q], 16 * (half + 1))
                        for m in range(BG // 2):
                            act.wait_ge(X["built"], B * BG + 2 * m + 2 + RG)
                            act.activation(AT[:, q, :, 2 * m * G:2 * m * G + 2 * G],
                                           bank[m % NAB][:, 0:2 * CW].rearrange("p (d h) -> p h d", h=HI), ACT.Copy).then_inc(X["ev"], 1)

                    if k == 0:
                        for q in range(2):
                            act.nop().then_inc(at_stored[q], 16)
                        with act.Fori(0, NB // 2) as i:
                            for q in range(2):
                                block(2 * i + q, q, i)
                        block(NB - 1, 0, NB // 2)
                    else:
                        act.nop().then_inc(s("act_passed"), 1)
                with act.Else():
                    act.nop().then_inc(s("act_passed"), 1)
            act.wait_ge(ph[0]["var"], 1)
            act.activation(rstd[:], mv[:, :, 1], ACT.Sqrt, bias=epst[:, 0:1]).then_inc(ph[0]["rs"], 1)

        @block.tensor
        def _(pe):
            pe.wait_ge(s("consts"), 2)
            pe.wait_ge(s("part_ready"), 1)
            pe.matmul(bank[7][0:1, 0:NT + 2], ones[0:EP, 0:1], part[0:EP, :], start=True, stop=True).then_inc(s("cnt_ps"), 1)
            pe.wait_ge(s("ld_w"), 16 * 14)
            for j in range(3):
                m = pe.matmul(bank[4][:, j:j + 1], wfc[:, j * D:(j + 1) * D], w2[:, 0:1], start=True, stop=True)
            m.then_inc(s("v3_ready"), 1)
            pe.transpose(bank[5][:, 0:P], embr[:, 0, :], ident[:])
            pe.transpose(bank[5][:, P:R], embr[0:R - P, 1, :], ident[0:R - P, 0:R - P]).then_inc(s("emb_t"), 1)
            pe.wait_ge(s("vrb_ready"), 1)
            pe.matmul(bank[6][:, 0:R], vrb[:], embT[:], start=True, stop=True).then_inc(s("rrow_ps"), 1)

            def node_phase(k, rhs, width):
                with pe.Fori(0, PAIRS) as i:
                    for q in range(2):
                        pe.wait_ge(ph[k]["staged"], 2 * i + q + 1)
                        pe.transpose(bank[q][:, 0:P], stage[:, q, :], ident[:]).then_inc(ph[k]["tp"], 1)
                    for q in range(2):
                        pe.wait_ge(ph[k]["xt"], 2 * i + q + 1)
                        pe.wait_ge(ph[k]["nd"], 2 * i + q + 1)
                        pe.matmul(bank[2 + q][:, 0:width], nT[:, q, :], rhs, start=True, stop=True).then_inc(ph[k]["mp"], 1)

            pe.wait_ge(s("vsd"), 1)
            pe.wait_ge(s("loads_x"), 16)
            node_phase(0, wloop[:], D + 2)
            pe.wait_ge(s("lowT"), 1)
            pe.transpose(bank[4][0:1, 0:P], lows[:, 0:1], ident[:]).then_inc(s("low_ps"), 1)
            pe.wait_ge(s("low_in"), 1)
            pe.matmul(bank[4][:, 256:257], ones[0:1, :], lows[0:1, 2:3], start=True, stop=True).then_inc(s("low_ps"), 1)
            pe.wait_ge(s("nb_ready"), 1)
            nb = pe.value_load(plan_i[0:1, NT:NT + 1], min_val=1, max_val=NBMAX)

            with windows(pe, nb) as (i, b, n):
                for p in range(2):
                    t = 2 * n + p
                    for c in range(C):
                        g = c // TGRP
                        if c % TGRP == 0:
                            pe.wait_ge(s("mt_done"), t * NTG + g + 1)
                        pe.wait_ge(s("mask_ready"), t * C + c + 1)
                        m = pe.transpose(bank[g % 2][:, :].bitcast(BF16)[:, (c % TGRP) * P:(c % TGRP + 1) * P], hotb[:, c, :], identb[:])
                        if c % TGRP == TGRP - 1 or c == C - 1:
                            m.then_inc(s("tr_ready"), 1)
                        m = pe.matmul(bank[4][:, 0:R], hotb[:, c, :], toh[:, c, :], start=(c == 0), stop=(c == C - 1))
                    m.then_inc(s("c_ready"), 1)
                    pe.wait_ge(s("up_ready"), t + 1)
                    pe.transpose(bank[2][:, 256:256 + P], up[:], ident[:]).then_inc(s("upT_ps"), 1)
                    pe.wait_ge(s("upT_ready"), t + 1)
                    for g in range(NG):
                        w = min(GRP, C - g * GRP)
                        pe.wait_ge(s("mx_done"), t * NG + g + 1)
                        for c in range(g * GRP, g * GRP + w):
                            m = pe.matmul(bank[6 + g % 2][:, (c % GRP) * P:(c % GRP + 1) * P], ident[0:C, c:c + 1].broadcast_to([C, P]),
                                          upT[:], start=True, stop=True)
                        m.then_inc(s("u_ready"), 1)
                    pe.wait_ge(s("bm_ready"), t + 1)
                    for c in range(C):
                        m = pe.matmul(bank[2][:, 6 * c:6 * c + 6], hotT[:, c, :], bm3[:, :, :], start=True, stop=True)
                    m.then_inc(s("lk_ready"), 1)
                    for c in range(C):
                        pe.wait_ge(s("wm_ready"), t * C + c + 1)
                        m = pe.matmul(bank[3][:, 0:D + 2], hot[:, c, :], rows[:, p, c, 0:D + 2], start=(c == 0), stop=(c == C - 1))
                    m.then_inc(s("acc_ready"), 1)
                    pe.wait_ge(s("cc_ready"), t + 1)
                    pe.wait_ge(s("er_done"), t + 1)
                    pe.transpose(bank[5][:, 0:P], cacc[:, p, 0:P], ident[:])
                    pe.transpose(bank[5][0:R - P, P:2 * P], cacc[:, p, P:R], ident[:]).then_inc(s("ct_ready"), 1)
                    pe.wait_ge(s("ctc_ready"), 2 * t + 2)
                    pe.matmul(bank[5][:, 2 * P:3 * P], relr[:, 0, :], cT[:, 0, :], start=True, stop=False)
                    pe.matmul(bank[5][:, 2 * P:3 * P], relr[0:R - P, 1, :], cT[0:R - P, 1, :], start=False, stop=True).then_inc(s("er_ready"), 1)

            pe.wait_ge(s("deg_ready"), 1)
            pe.matmul(bank[7][:, 0:NT], tri[0:TN, :], degt[0:TN, :], start=True, stop=True)
            pe.matmul(bank[7][:, 64:64 + NT], ones[0:TN, :], degt[0:TN, :], start=True, stop=True).then_inc(s("pre_ps"), 1)
            pe.wait_ge(s("rp_ready"), 1)
            pe.wait_ge(s("er_done"), nb * NT + 1)
            pe.transpose(bank[6][:, 0:P], tmp[:, 0, :], ident[:]).then_inc(s("rpT"), 1)
            pe.wait_ge(s("ok_ps"), 1)
            pe.matmul(bank[6][0:1, 256:257], ones[:, 0:1], fin[:, 0:1], start=True, stop=True).then_inc(s("ok_ps"), 1)
            node_phase(1, wself[:, 0, :], 2 * D)
            for b in range(NGB):
                pe.wait_ge(s("wT_ready"), b + 1)
                if b >= 2:
                    pe.wait_ge(s("idx_done"), b - 1)
                for m in range(2 * GC):
                    r = pe.transpose(bank[4 + b % 2][:, m * P:(m + 1) * P],
                                     recc[:, b % 2, m // GC, (m % GC) * P:(m % GC + 1) * P], ident[:])
                r.then_inc(s("wT_ps"), 1)
            pe.wait_ge(s("ok_ready"), 1)
            ok = pe.value_load(ok_i[0:1, 0:1], min_val=0, max_val=1)
            for k in range(2):
                if k == 1:
                    node_phase(2, wself[:, 1, :], 2 * D)
                with pe.If(ok):
                    X = dense[k]
                    pe.wait_ge(ph[k + 1]["mp"], NT)
                    pe.wait_ge(ph[k + 1]["nd"], NT + 2)

                    def build(B, g):
                        m, half = g // 2, g % 2
                        pe.wait_ge(X["oh"], B * BG + g + 1)
                        if half == 0:
                            pe.wait_ge(X["ev"], B * (BG // 2) + m + 1)
                        for c in range(GC):
                            r = pe.matmul(bank[m % NAB][:, half * CW:(half + 1) * CW], ohl[:, g % RG, c, :], ohm[:, g % RG, c, :],
                                          start=(c == 0), stop=(c == GC - 1))
                        r.then_inc(X["built"], 1)

                    def product(B, q, h):
                        if h == 0 and k == 0:
                            pe.wait_ge(X["ev"], (B + 1) * (BG // 2) + NAB)
                        for j in range(3):
                            r = pe.matmul(bank[5 + q][:, 0:BD], hs[0:TN, j, h, :], AT[0:TN, q, h, :],
                                          start=(h == 0 and j == 0), stop=(h == HI - 1 and j == 2))
                        if h == HI - 1:
                            r.then_inc(X["dn"], 1)

                    def project(B):
                        pe.wait_ge(X["st"], B + 1)
                        for hh in range(2):
                            r = pe.matmul(bank[7][0:TN, hh * D:(hh + 1) * D], sT[:, hh * TN:(hh + 1) * TN], wr[:, k, :],
                                          start=True, stop=True)
                        r.then_inc(X["ou"], 1)

                    def block(B, q, before):
                        for g in range(BG + LEAD):
                            if g < BG:
                                build(B, g)
                            if g == 12 and before >= 2:
                                project(B - 2)
                            if g >= LEAD and before >= 1:
                                product(B - 1, 1 - q, g - LEAD)

                    if k == 0:
                        block(0, 0, 0)
                        pe.wait_ge(X["split"], 1)
                        block(1, 1, 1)
                        with pe.Fori(1, NB // 2) as i:
                            for q in range(2):
                                block(2 * i + q, q, 2)
                        block(NB - 1, 0, 2)
                        for h in range(HI):
                            product(NB - 1, 0, h)
                        project(NB - 2)
                        project(NB - 1)
                    else:
                        def loaded_block(B, q, half, before=True):
                            pe.wait_ge(at_loaded[q], 16 * (half + 1))
                            for h in range(HI):
                                product(B, q, h)
                                if h == 12 and before:
                                    project(B - 1)

                        pe.wait_ge(X["split"], 1)
                        loaded_block(0, 0, 0, False)
                        loaded_block(1, 1, 0)
                        with pe.Fori(1, NB // 2) as i:
                            for q in range(2):
                                loaded_block(2 * i + q, q, i)
                        loaded_block(NB - 1, 0, NB // 2)
                        project(NB - 1)
                with pe.Else():
                    L = lay[k]
                    with windows(pe, nb) as (i, b, n):
                        for p in range(2):
                            t = 2 * n + p
                            for c in range(C):
                                if c % HC == 0:
                                    pe.wait_ge(L["gath"][p][c // HC], (n + 1) * (16 * HC))
                                pe.wait_ge(L["hot_ready"], t * C + c + 1)
                                m = pe.matmul(bank[3 + p][:, 0:D], hot[:, c, :], rows[:, p, c, 0:D], start=(c == 0), stop=(c == C - 1))
                            m.then_inc(L["acc_ready"], 1)
                            pe.wait_ge(L["s_ready"], t + 1)
                            pe.transpose(bank[5][:, 0:P], agg[:], ident[:]).then_inc(L["sT_ready"], 1)
                            pe.wait_ge(L["sTc_ready"], t + 1)
                            pe.matmul(bank[6][0:TN, 0:D], sT[:, 0:TN], wr[:, k, :], start=True, stop=True).then_inc(L["o_ready"], 1)

        @block.vector
        def _(v):
            ch = Chain(v, s("dve_seq"), s("dve_passed"))
            link, link_alone = ch.link, ch.link_alone
            v.memset(xs[96:P, :, :], 0.0).then_inc(s("xs_zero"), 1)
            v.memset(ones[:], 1.0).then_inc(s("consts"), 1)
            v.memset(epst[:], EPS)
            v.memset(later[:], 1.0)
            v.memset(acc[:], 0.0)
            v.memset(cacc[:], 0.0)
            v.memset(mrun[:], 0.0)
            v.memset(tmp[:], 0.0)
            v.memset(up[:], 0.0)
            v.memset(lows[:], 0.0)
            v.memset(cT[:], 0.0)
            link(v.memset(part[:], 0.0))
            v.memset(later[:, 0:1], 0.0)
            v.wait_ge(s("iotas"), 4)
            v.tensor_copy(iota[:], iota_i[:])
            v.tensor_copy(iotab[:], iota_i[:])
            v.tensor_copy(jw[:], jw_i[:])
            v.tensor_copy(kcol[:], kcol_i[:])
            link(v.tensor_copy(thr[:], thr_i[:]))

            v.wait_ge(s("ld_dst"), 16)
            smp = scr[0:EP, 0:NS]
            cmp = scr[0:EP, 64:64 + (NT + 1) * NS].rearrange("p (t m) -> p t m", m=NS)
            link(v.tensor_copy(smp, dall[0:EP, 0:EW:SAMP]))
            link(v.tensor_tensor(cmp, scr[0:EP, 0:NS][:, None, :].broadcast_to([EP, NT + 1, NS]),
                                 thr[0:EP, :][:, :, None].broadcast_to([EP, NT + 1, NS]), ALU.is_lt))
            link(v.tensor_reduce(part[0:EP, 0:NT + 1], cmp, AX, ALU.add))
            v.wait_ge(s("ld_next"), 16)
            viol = scr[0:EP, 4096:4096 + EW]
            link(v.tensor_tensor(viol, dall[0:EP, 0:EW], dall[0:EP, EW:2 * EW], ALU.is_gt))
            v.tensor_reduce(part[0:EP, NT + 1:NT + 2], viol, AX, ALU.add).then_inc(s("part_ready"), 1)
            v.wait_ge(s("cnt_ps"), 1)
            cnt, base, need = plan[0:1, 0:NT + 2], plan2[0:1, 0:NT], plan[0:1, 0:NT]
            link(v.tensor_copy(plan[0:1, 0:NT + 2], bank[7][0:1, 0:NT + 2]))
            link(v.tensor_scalar(plan2[0:1, 56:57], plan[0:1, NT + 1:NT + 2], 0.0, None, ALU.is_equal))
            link(v.tensor_scalar(base, plan[0:1, 0:NT], float(SAMP), -float(SAMP), ALU.mult, ALU.add))
            link(v.tensor_scalar(base, base, 0.0, plan2[0:1, 56:57], ALU.max, ALU.mult))
            v.tensor_scalar(plan2[0:1, 57:58], plan2[0:1, 56:57], -2.0 * E, 2.0 * E, ALU.mult, ALU.add)
            link(v.scalar_tensor_tensor(part[0:1, 0:NT], plan[0:1, 1:NT + 1], float(SAMP), base, ALU.mult, ALU.subtract))
            link(v.tensor_reduce(plan2[0:1, 58:59], part[0:1, 0:NT], AX, ALU.max))
            link(v.tensor_tensor(plan2[0:1, 59:60], plan2[0:1, 58:59], plan2[0:1, 57:58], ALU.max))
            link(v.tensor_scalar(part[0:1, 0:NBMAX], jw[0:1, :], plan2[0:1, 59:60], None, ALU.is_lt))
            link(v.tensor_reduce(plan2[0:1, NT:NT + 1], part[0:1, 0:NBMAX], AX, ALU.add))
            v.tensor_copy(plan_i[0:1, 0:NT + 1], plan2[0:1, 0:NT + 1]).then_inc(s("nb_ready"), 1)
            v.wait_ge(s("nb_ready"), 1)
            nb = v.value_load(plan_i[0:1, NT:NT + 1], min_val=1, max_val=NBMAX)

            v.wait_ge(s("ld_src"), 16)
            flat = ys[0:EP, :, :].rearrange("p a b -> p (a b)")
            srci, q_i = flat[:, 0:EW].bitcast(I32), flat[:, EW:2 * EW].bitcast(I32)
            qf, lo, off = flat[:, 2 * EW:3 * EW], flat[:, 3 * EW:4 * EW], hotf[0:EP, 0:EW]
            v.wait_ge(s("edges"), 96)
            link(v.tensor_scalar(qf, srci, 1.0 / TN, -0.496, ALU.mult, ALU.add))
            link(v.tensor_copy(q_i, qf))
            link(v.tensor_copy(qf, q_i))
            link(v.scalar_tensor_tensor(lo, qf, -float(TN), srci, ALU.mult, ALU.add))
            link(v.tensor_scalar(off, lo, 0.0, None, ALU.is_lt))
            link(v.tensor_tensor(qf, qf, off, ALU.subtract))
            link(v.tensor_scalar(off, lo, float(TN), None, ALU.is_ge))
            link(v.tensor_tensor(qf, qf, off, ALU.add))
            v.scalar_tensor_tensor(recs[0:EP, :, GRAN:2 * GRAN], qf.rearrange("p (j r) -> p j r", r=GRAN), -float(TN),
                                   srci.rearrange("p (j r) -> p j r", r=GRAN), ALU.mult, ALU.add)
            v.scalar_tensor_tensor(recs[0:EP, :, 0:GRAN], dall[0:EP, 0:EW].rearrange("p (j r) -> p j r", r=GRAN), float(HI),
                                   qf.rearrange("p (j r) -> p j r", r=GRAN), ALU.mult, ALU.add).then_inc(s("recs_ready"), 1)

            v.wait_ge(s("v3_ready"), 1)
            link(v.tensor_copy(v3[:], bank[4][:, 0:3]))
            v.wait_ge(s("emb_t"), 1)
            v.tensor_copy(wloop[:, D:D + 2], v3[:, 0:2]).then_inc(s("vsd"), 1)
            link(v.tensor_copy(embT[:], bank[5][:, 0:R]))
            v.tensor_scalar(vrb[:], ones[:], v3[:, 2:3], None, ALU.mult).then_inc(s("vrb_ready"), 1)
            v.wait_ge(s("rrow_ps"), 1)
            link(v.tensor_copy(rrow[:], bank[6][:, 0:R]))
            v.wait_ge(s("loads_x"), 16)
            v.memset(ssd[:], 0.0)
            v.memset(xs[:, :, D + 1:D + 2], 1.0)
            link(v.memset(xs[:, :, D + 2:HW], 0.0))
            for k in range(3):
                v.nop().then_inc(ph[k]["nd"], 2)
            v.nop().then_inc(s("mx_done"), 2)
            v.nop().then_inc(s("rv_done"), 2)
            v.nop().then_inc(s("er_done"), 1)
            v.nop().then_inc(s("mt_done"), 2)
            with v.Fori(0, PAIRS) as i:
                for q in range(2):
                    v.wait_ge(ph[0]["mp"], 2 * i + q + 1)
                    v.tensor_tensor(at(res, q, i), xs[:, bass.ds(2 * i + q, 1), 0:D].rearrange("p a f -> p (a f)"),
                                    bank[2 + q][:, 0:D], ALU.add)
                    v.tensor_copy(at(ssd, q, i), bank[2 + q][:, D:D + 2])
                    v.tensor_copy(xs[:, bass.ds(2 * i + q, 1), D:D + 1].rearrange("p a f -> p (a f)"),
                                  bank[2 + q][:, D:D + 1]).then_inc(ph[0]["nd"], 1)
            v.wait_ge(ph[0]["nd"], NT + 2)
            v.tensor_reduce(lows[:, 0:1], ssd[:, :, 0], AX, ALU.min).then_inc(s("lowT"), 1)
            v.tensor_reduce(lows[0:1, 3:4], rrow[0:1, :], AX, ALU.min)
            v.wait_ge(s("low_ps"), 1)
            link(v.tensor_reduce(lows[0:1, 1:2], bank[4][0:1, 0:P], AX, ALU.min))
            v.tensor_tensor(lows[0:1, 2:3], lows[0:1, 1:2], lows[0:1, 3:4], ALU.add).then_inc(s("low_in"), 1)
            v.wait_ge(s("low_ps"), 2)
            link(v.tensor_copy(low[:, 0:1], bank[4][:, 256:257]))
            link(v.tensor_scalar(low[:, 1:2], low[:, 0:1], -1.0, None, ALU.add))

            v.tensor_copy(identb[:], ident[:])

            def prepare(p, n, t, tile):
                v.wait_ge(win[p], (n + 1) * 48)
                link(v.tensor_copy(etf[:], etw[:, p, :]))
                for c in range(C):
                    r = v.tensor_scalar(toh[:, c, :], iotab[:, 0:R], etf[:, c:c + 1], None, ALU.is_equal)
                link(r)
                for c in range(C):
                    v.wait_ge(s("rv_done"), t * C + c + 1)
                    v.tensor_tensor_reduce(junk[:, c % 2, :], toh[:, c, :], rrow[:], 1.0, 0.0, ALU.mult, ALU.add,
                                           rv[:, c:c + 1]).then_inc(s("rv_done"), 1)
                v.wait_ge(s("rv_done"), (t + 1) * C + 2)
                if not isinstance(t, int):
                    v.wait_ge(s("wm_ready"), t * C)
                link(v.tensor_scalar(dl[:], dstw[:, p, :], thr[:, tile], None, ALU.subtract))
                for c in range(C):
                    v.tensor_scalar(hotb[:, c, :], iotab[:, 0:P], dl[:, c:c + 1], None, ALU.is_equal).then_inc(s("mask_ready"), 1)

            prepare(0, 0, 0, slice(0, 1))
            LINKS = 2 * L0_LINKS
            with windows(v, nb) as (i, b, n), ch.turns(n, LINKS, nb * PAIRS):
                for p in range(2):
                    t = 2 * n + p
                    for j in range(2):
                        v.wait_ge(gath[p][j], (n + 1) * (16 * HC))
                        cs = slice(j * HC, (j + 1) * HC)
                        link(v.tensor_tensor(u[:, cs], rows[:, p, cs, D], rv[:, cs], ALU.add))
                        link(v.tensor_scalar(up[:, cs], u[:, cs], low[:, 0:1], 1.0, ALU.subtract, ALU.add))
                    v.nop().then_inc(s("up_ready"), 1)
                    v.wait_ge(s("upT_ps"), t + 1)
                    v.tensor_copy(upT[:], bank[2][0:C, 256:256 + P]).then_inc(s("upT_ready"), 1)
                    for g in range(NG):
                        w = min(GRP, C - g * GRP)
                        v.wait_ge(s("mt_done"), t * NTG + (g * GRP + w - 1) // TGRP + 3)
                        v.wait_ge(s("u_ready"), t * NG + g + 1)
                        v.nop().then_inc(s("dve_passed"), 1)
                        v.tensor_tensor_reduce(hot[:, g * GRP:g * GRP + w, :], hotT[:, g * GRP:g * GRP + w, :],
                                               bank[6 + g % 2][:, 0:w * P].rearrange("p (c e) -> p c e", e=P), 1.0, 0.0,
                                               ALU.mult, ALU.max, gmax[:, g:g + 1]).then_inc(s("mx_done"), 1)
                    v.wait_ge(s("mx_done"), t * NG + NG + 2)
                    bt = ssd[:, bass.ds(2 * i + p, 1), 1:2].rearrange("p a f -> p (a f)")
                    first = later[:, bass.ds(b, 1)]

                    def max_of(o, top):
                        link(v.scalar_tensor_tensor(mold[:, 2:3], top, low[:, 1:2], bt, ALU.add, ALU.add))
                        link(v.scalar_tensor_tensor(o, mold[:, 2:3], 0.01, mold[:, 2:3], ALU.mult, ALU.max))

                    link(v.tensor_reduce(bmax[:], gmax[:], AX, ALU.max))
                    max_of(mold[:, 0:1], mrun[:, p:p + 1])
                    link(v.scalar_tensor_tensor(mrun[:, p:p + 1], mrun[:, p:p + 1], first, bmax[:], ALU.mult, ALU.max))
                    max_of(bm[:, 1:2], mrun[:, p:p + 1])
                    v.nop().then_inc(s("dve_passed"), 1)
                    link(v.tensor_copy(bm[:, 0:1], bt))
                    link(v.tensor_copy(bm3[:, 0, :], bm[:]))
                    link(v.tensor_tensor(bmr[:, 0, :], bm[:], bm3[:, 0, :], ALU.subtract))
                    link(v.tensor_copy(bm3[:, 1, :], bmr[:, 0, :]))
                    link(v.tensor_tensor(bmr[:, 1, :], bmr[:, 0, :], bm3[:, 1, :], ALU.subtract))
                    v.tensor_copy(bm3[:, 2, :], bmr[:, 1, :]).then_inc(s("bm_ready"), 1)
                    v.tensor_tensor(z[:, C:C + 1], mold[:, 0:1], bm[:, 1:2], ALU.subtract)
                    v.wait_ge(s("lk_ready"), t + 1)
                    look3 = bank[2][:, 0:6 * C].rearrange("p (c j k) -> p c j k", j=3, k=2)
                    link(v.tensor_copy(look[:], look3[:, :, 0, :]))
                    link(v.tensor_tensor(look[:], look[:], look3[:, :, 1, :], ALU.add))
                    link(v.tensor_tensor(look[:], look[:], look3[:, :, 2, :], ALU.add))
                    link(v.tensor_tensor(z[:, 0:C], u[:], look[:, :, 0], ALU.add))
                    link(v.scalar_tensor_tensor(z2[:], z[:, 0:C], 0.01, z[:, 0:C], ALU.mult, ALU.max))
                    link(v.tensor_tensor(z[:, 0:C], z2[:], look[:, :, 1], ALU.subtract))
                    v.tensor_scalar(z[:], z[:], 1.0, None, ALU.min).then_inc(s("d_ready"), 1)
                    v.wait_ge(s("c_ready"), t + 1)
                    link(v.scalar_tensor_tensor(cacc[:, p, :], cacc[:, p, :], first, bank[4][:, 0:R], ALU.mult, ALU.add))
                    v.nop().then_inc(s("cc_ready"), 1)
                    if p == 0:
                        prepare(1, n, t + 1, bass.ds(2 * i + 1, 1))
                    else:
                        prepare(0, n + 1, t + 1, bass.ds(2 * nc.s_assert_within(i + (b + 1) // nb, 0, PAIRS), 1))
                    v.wait_ge(s("acc_ready"), t + 1)
                    v.nop().then_inc(win_free[p], 1)
                    link(v.tensor_tensor(fin[:, 0:1], wexp[:, C:C + 1], first, ALU.mult))
                    link(v.scalar_tensor_tensor(acc[:, p, 0:D + 2], acc[:, p, 0:D + 2], fin[:, 0:1], bank[3][:, 0:D + 2], ALU.mult, ALU.add))
                    deg, has, no, den, rec = (fin[:, j:j + 1] for j in range(1, 6))
                    link(v.tensor_reduce(deg, cacc[:, p, :], AX, ALU.add))
                    v.tensor_scalar(has, deg, 0.0, None, ALU.is_gt)
                    link(v.tensor_scalar(no, deg, 0.0, None, ALU.is_equal))
                    one = lambda a: a[:, bass.ds(2 * i + p, 1)]
                    v.tensor_scalar(one(degs), deg, 1.0, None, ALU.max)
                    v.tensor_copy(one(degt), deg)
                    v.tensor_copy(one(niso), has)
                    v.tensor_copy(one(iso), no)
                    link(v.tensor_tensor(den, acc[:, p, D + 1:D + 2], no, ALU.add))
                    link(v.reciprocal(rec, den))
                    link(v.tensor_tensor(rec, rec, has, ALU.mult))
                    link(v.scalar_tensor_tensor(agg[:], acc[:, p, 0:D], rec, at(res, p, i), ALU.mult, ALU.add))
                    link_alone(v.scalar_tensor_tensor(agg[:], xs[:, bass.ds(2 * i + p, 1), 0:D].rearrange("p a f -> p (a f)"), no, agg[:],
                                                ALU.mult, ALU.add))
                    v.tensor_copy(at(ys, p, i), agg[:])
                    link_alone(v.bn_stats(stat[:], agg[:]))
                    link_alone(v.bn_aggr(fin[:, 6:8], stat[:]))
                    link_alone(v.tensor_copy(at(mv, p, i), fin[:, 6:8]))
            v.nop().then_inc(ph[1]["var"], 2)
            v.nop().then_inc(s("deg_ready"), 1)

            v.memset(part[0:1, :], float(E)).then_inc(s("st_pad"), 1)
            v.wait_ge(s("pre_ps"), 1)
            incl, rp = tmp[:, 1, 0:NT], tmp[:, 0, 0:NT]
            link(v.tensor_tensor_scan(incl, ones[:, 0:NT], bank[7][:, 64:64 + NT], 0.0, ALU.mult, ALU.add))
            link(v.tensor_tensor(incl, incl, bank[7][:, 64:64 + NT], ALU.subtract))
            v.tensor_tensor(rp, incl, bank[7][:, 0:NT], ALU.add).then_inc(s("rp_ready"), 1)
            v.wait_ge(s("rpT"), 1)
            v.tensor_copy(sT[0:NT, 0:TN // G], bank[6][0:NT, 0:TN:G]).then_inc(s("rpT_ready"), 1)
            v.wait_ge(s("gst_loaded"), 32)
            gif, cover = u[:, 0:NGB], u[:, NGB:2 * NGB]
            link(v.tensor_copy(gst_i[:, 0, :], gstf[:, 0, :]))
            link(v.tensor_scalar(gst_i[:, 1, :], gst_i[:, 0, :], GRAN.bit_length() - 1, None, ALU.logical_shift_right))
            link(v.tensor_copy(gif, gst_i[:, 1, :]))
            for j in range(GW):
                r = v.tensor_scalar(gidx[:, j, :], gif, float(j), None, ALU.add)
            r.then_inc(s("gi_ready"), 1)
            link(v.scalar_tensor_tensor(cover, gif, -float(GRAN), gstf[:, 1, :], ALU.mult, ALU.add))
            link(v.tensor_scalar(cover, cover, float(GW * GRAN), None, ALU.is_gt))
            v.tensor_reduce(fin[:, 0:1], cover, AX, ALU.add).then_inc(s("ok_ps"), 1)
            v.wait_ge(s("ok_ps"), 2)
            link(v.tensor_scalar(plan2[0:1, 61:62], bank[6][0:1, 256:257], 0.0, plan2[0:1, 56:57], ALU.is_equal, ALU.mult))
            v.tensor_copy(ok_i[:], plan2[0:1, 61:62]).then_inc(s("ok_ready"), 1)

            def layer_norm(k):
                v.wait_ge(ph[k]["rs"], 2 if k == 1 else 1)
                if k == 1:
                    v.reciprocal(norm[:], norm[:])
                link_alone(v.reciprocal(rstd[:], rstd[:]))
                with v.Fori(0, PAIRS) as i:
                    for q in range(2):
                        tl = bass.ds(2 * i + q, 1)
                        v.tensor_scalar(at(ys, q, i), at(ys, q, i), mv[:, tl, 0:1].rearrange("p a f -> p (a f)"), rstd[:, tl],
                                        ALU.subtract, ALU.mult).then_inc(ph[k]["nsrc"], 1)

            def self_messages(k):
                with v.Fori(0, PAIRS) as i, ch.turns(i, 2, PAIRS):
                    for q in range(2):
                        tl = bass.ds(2 * i + q, 1)
                        v.wait_ge(ph[k + 1]["mp"], 2 * i + q + 1)
                        link(v.tensor_scalar(tmp[:, q, :], bank[2 + q][:, D:2 * D], niso[:, tl], None, ALU.mult))
                        v.scalar_tensor_tensor(at(res, q, i), bank[2 + q][:, 0:D], iso[:, tl], tmp[:, q, :],
                                               ALU.mult, ALU.add).then_inc(ph[k + 1]["nd"], 1)
                v.wait_ge(ph[k + 1]["nd"], NT + 2)

            layer_norm(1)
            self_messages(0)
            for b in range(NGB):
                v.wait_ge(wgat[b], 16 * GW)
                if b >= 2:
                    v.wait_ge(s("wT_ps"), b - 1)
                for m in range(2):
                    w = recw[:, b, :, m * GRAN:(m + 1) * GRAN]
                    o = recc[:, b % 2, m, :].rearrange("p (j r) -> p j r", r=GRAN)
                    r = v.tensor_scalar(o, w, kcol[:, b:b + 1], None, ALU.subtract) if m == 0 else v.tensor_copy(o, w)
                r.then_inc(s("wT_ready"), 1)
            v.wait_ge(s("idx_done"), NGB)
            ok = v.value_load(ok_i[0:1, 0:1], min_val=0, max_val=1)

            def dense_layer(k):
                X = dense[k]
                dc = Chain(v, X["seq"], s("dve_passed"))
                if k == 0:
                    v.nop().then_inc(X["built"], RG)
                    v.nop().then_inc(X["ev"], NAB)
                v.nop().then_inc(X["dn"], 2)
                v.nop().then_inc(X["x1_free"], 2)
                for j in range(0, NT, 5):
                    part_ = slice(j, j + 5)
                    dc.link(v.tensor_copy(hs[:, 0, part_, :], ys[:, part_, :]))
                    dc.link(v.tensor_tensor(rem[:], ys[:, part_, :], hs[:, 0, part_, :], ALU.subtract))
                    dc.link(v.tensor_copy(hs[:, 1, part_, :], rem[:]))
                    dc.link(v.tensor_tensor(hs[:, 2, part_, :], rem[:], hs[:, 1, part_, :], ALU.subtract))
                v.nop().then_inc(X["split"], 1)

                def one_hots(B, q, g):
                    v.wait_ge(X["built"], B * BG + g + 1)
                    for c in range(GC):
                        v.tensor_scalar(ohm[:, g % RG, c, :], iotab[:, 0:CW], idxf[:, q, c, g:g + 1], None, ALU.is_equal)
                        r = v.tensor_scalar(ohl[:, g % RG, c, :], iotab[:, 0:P], idxf[:, q, GC + c, g:g + 1], None, ALU.is_equal)
                    r.then_inc(X["oh"], 1)

                def sums(B, q):
                    v.wait_ge(X["dn"], B + 3)
                    v.tensor_tensor(sT[:], bank[5 + q][:, 0:BD], erT[:, bass.ds(B * BD, BD)], ALU.add).then_inc(X["st"], 1)

                def finish(B, q):
                    tl = bass.ds(B * 2, 2)
                    t2 = tmp[0:TN, :, :]
                    v.wait_ge(X["ou"], B + 1)
                    dc.link(v.tensor_tensor(t2, bank[7][0:TN, 0:2 * D].rearrange("p (h f) -> p h f", h=2),
                                            norm[0:TN, tl][:, :, None].broadcast_to([TN, 2, D]), ALU.mult))
                    dc.link(v.tensor_tensor(t2, t2, res[0:TN, tl, :], ALU.add))
                    if k == 0:
                        dc.link(v.scalar_tensor_tensor(ys[0:TN, tl, :], t2, SLOPE, t2, ALU.mult, ALU.max))
                        return
                    t3 = x1r[0:TN, q, :, :]
                    dc.link(v.scalar_tensor_tensor(t2, t2, SLOPE, t2, ALU.mult, ALU.max))
                    v.wait_ge(X["x1"][q], B_count(B, q))
                    dc.link(v.tensor_tensor(t2, t2, t3, ALU.add))
                    v.nop().then_inc(X["x1_free"], 1)
                    v.tensor_scalar(ys[0:TN, tl, :], t2, 1.0, None, ALU.mult)
                    for hh in range(2):
                        dc.link_alone(v.bn_stats(stat[0:TN, :], tmp[0:TN, hh, :]))
                        dc.link_alone(v.bn_aggr(fin[0:TN, 6:8], stat[0:TN, :]))
                        dc.link_alone(v.tensor_copy(mv[0:TN, bass.ds(B * 2 + hh, 1), :].rearrange("p a f -> p (a f)"), fin[0:TN, 6:8]))

                def B_count(B, q):
                    return (turn_of(B) + 1) * 16

                def turn_of(B):
                    return B // 2 if isinstance(B, int) else halves[0]

                halves = [None]

                def block(B, q, before, half_before=None):
                    dc.link_alone(v.tensor_copy(idxf[:, q, :, :], idx[:, :, bass.ds(B * BG, BG)]))
                    for g in range(BG):
                        one_hots(B, q, g)
                        if before >= 2 and g == 4:
                            sums(B - 2, q)
                        if before >= 2 and g == 20:
                            halves[0] = half_before
                            finish(B - 2, q)

                if k == 1:
                    def loaded_block(B, q, half):
                        halves[0] = half
                        sums(B, q)
                        finish(B, q)

                    with v.Fori(0, NB // 2) as i, dc.turns(i, 2 * 10, NB // 2):
                        for q in range(2):
                            loaded_block(2 * i + q, q, i)
                    loaded_block(NB - 1, 0, NB // 2)
                    return
                block(0, 0, 0)
                block(1, 1, 1)
                each = 2 * (1 + 3)
                with v.Fori(1, NB // 2) as i, dc.turns(i - 1, each, NB // 2 - 1):
                    for q in range(2):
                        block(2 * i + q, q, 2, i - 1)
                block(NB - 1, 0, 2)
                for B, q in ((NB - 2, 1), (NB - 1, 0)):
                    sums(B, q)
                    finish(B, q)

            def gathered_layer(k):
                L = lay[k]
                gc = Chain(v, dense[k]["seq"], s("dve_passed"))
                with windows(v, nb) as (i, b, n), gc.turns(n, 2 * (4 + 4 * k), nb * PAIRS):
                    for p in range(2):
                        t = 2 * n + p
                        tl = bass.ds(2 * i + p, 1)
                        v.wait_ge(L["win"][p], (n + 1) * (48 + 16 * k))
                        gc.link(v.tensor_scalar(dl[:], dstw[:, p, :], thr[:, tl], None, ALU.subtract))
                        for c in range(C):
                            v.tensor_scalar(hot[:, c, :], iota[:, 0:P], dl[:, c:c + 1], None, ALU.is_equal).then_inc(L["hot_ready"], 1)
                        v.wait_ge(L["acc_ready"], t + 1)
                        gc.link(v.scalar_tensor_tensor(acc[:, p, 0:D], acc[:, p, 0:D], later[:, bass.ds(b, 1)], bank[3 + p][:, 0:D],
                                                       ALU.mult, ALU.add))
                        v.tensor_copy(agg[:], acc[:, p, 0:D]).then_inc(L["s_ready"], 1)
                        v.wait_ge(L["sT_ready"], t + 1)
                        v.tensor_tensor(sT[:, 0:TN], bank[5][:, 0:TN], erT[:, bass.ds((2 * i + p) * TN, TN)], ALU.add)\
                            .then_inc(L["sTc_ready"], 1)
                        v.wait_ge(L["o_ready"], t + 1)
                        t0, t1 = tmp[0:TN, 0, :], tmp[0:TN, 1, :]
                        yt = ys[0:TN, tl, :].rearrange("p a f -> p (a f)")
                        gc.link(v.scalar_tensor_tensor(t0, bank[6][0:TN, 0:D], norm[0:TN, tl],
                                                       res[0:TN, tl, :].rearrange("p a f -> p (a f)"), ALU.mult, ALU.add))
                        if k == 0:
                            gc.link(v.scalar_tensor_tensor(yt, t0, SLOPE, t0, ALU.mult, ALU.max))
                        else:
                            gc.link(v.scalar_tensor_tensor(t1, t0, SLOPE, t0, ALU.mult, ALU.max))
                            gc.link(v.tensor_tensor(t0, x1r[0:TN, p, 0, :], t1, ALU.add))
                            v.tensor_scalar(yt, t0, 1.0, None, ALU.mult)
                            gc.link_alone(v.bn_stats(stat[0:TN, :], t0))
                            gc.link_alone(v.bn_aggr(fin[0:TN, 6:8], stat[0:TN, :]))
                            gc.link_alone(v.tensor_copy(mv[0:TN, tl, :].rearrange("p a f -> p (a f)"), fin[0:TN, 6:8]))
                        v.nop().then_inc(L["win_free"][p], 1)

            for k in range(2):
                if k == 1:
                    v.nop().then_inc(ph[2]["nsrc"], NT)
                    self_messages(1)
                v.wait_ge(ph[k + 1]["stored"], 16)
                with v.If(ok):
                    dense_layer(k)
                with v.Else():
                    gathered_layer(k)
            v.nop().then_inc(ph[0]["var"], 1)
            layer_norm(0)
            v.wait_ge(ph[0]["nsrc"], NT)
            v.nop().then_inc(s("st_out"), 1)


_INS = ['x', 'src', 'dst', 'edge_type_200', 'L0_gnn_emb_rel', 'L0_gnn_loop_weight', 'L0_gnn_attn_fc_w', 'L0_gnn_attn_fc2_w',
        'L1_gnn_rel_embed', 'L1_gnn_W_r1', 'L1_gnn_W_sl1', 'L1_gnn_W_el1', 'L1_gnn_W_r2', 'L1_gnn_W_sl2', 'L1_gnn_W_el2']


def kernel(**inputs):
    import numpy as _np
    import concourse.bacc as _bacc
    from concourse import mybir as _mybir
    from concourse.bass_utils import run_bass_kernel_spmd as _run

    nc = _bacc.Bacc("TRN2", target_bir_lowering=False, num_devices=1)
    arrays, a = {}, {}
    for name in _INS:
        v = _np.ascontiguousarray(inputs[name])
        arrays[f"in_{name}_dram"] = v
        a[name] = nc.dram_tensor(f"in_{name}_dram", v.shape, _mybir.dt.from_np(v.dtype), kind="ExternalInput").ap()
    out = nc.dram_tensor("out_0_dram", (N, D), F32, kind="ExternalOutput").ap()
    build(nc, a['x'], a['src'], a['dst'], a['edge_type_200'], a['L0_gnn_emb_rel'], a['L0_gnn_loop_weight'],
          a['L0_gnn_attn_fc_w'], a['L0_gnn_attn_fc2_w'], a['L1_gnn_rel_embed'],
          [a['L1_gnn_W_r1'], a['L1_gnn_W_r2']], [a['L1_gnn_W_sl1'], a['L1_gnn_W_sl2']],
          [a['L1_gnn_W_el1'], a['L1_gnn_W_el2']], out)
    r = _run(nc, [arrays], core_ids=[0])
    return r.results[0]["out_0_dram"]
```
